# Optimizing a Trainium2 kernel written in Bass

```python
import numpy as np
import jax
import jax.numpy as jnp

def _softmax(x, axis=-1):
    return jax.nn.softmax(x, axis=axis)

def _gelu(x):
    return jax.nn.gelu(x, approximate=True)

def _silu(x):
    return jax.nn.silu(x)

def _sigmoid(x):
    return jax.nn.sigmoid(x)

def _layernorm(x, axis=-1, eps=1e-05):
    m = jnp.mean(x, axis=axis, keepdims=True)
    v = jnp.var(x, axis=axis, keepdims=True)
    return (x - m) / jnp.sqrt(v + eps)

def _scatter_add(tgt, idx, src, axis=0):
    return tgt.at[idx].add(src)

def _segment_sum(src, seg, n):
    return jax.ops.segment_sum(src, seg, n)
kernel_name = 'mk_decoder_preln_d1_seqx_r4_af5845'

def setup_inputs(seed: int=0):
    np.random.seed(seed)
    _w = jnp.asarray

    def _rec_inputs():
        import jax
        import jax.numpy as jnp
        _rk = jax.random.key(seed)
        x = -7.109e-05 + 0.9999 * jax.random.normal(jax.random.fold_in(_rk, 1), (8, 112, 1024), jnp.float32)
        _lenS = 112 - jax.random.randint(jax.random.fold_in(_rk, 7), (8,), 0, max(1, 112 // 4) + 1, jnp.int32)
        _lenS2 = 375 - jax.random.randint(jax.random.fold_in(_rk, 8), (8,), 0, max(1, 375 // 4) + 1, jnp.int32)
        _ctx_4096P = jax.random.normal(jax.random.fold_in(_rk, 11), (8, 16, 1024), jnp.float32)
        _ctx_4096c = jax.random.dirichlet(jax.random.fold_in(_rk, 511), 0.3 * jnp.ones((16,), jnp.float32), (8, 375))
        _ctx_4096t = jnp.einsum('bsk,bkd->bsd', _ctx_4096c, _ctx_4096P)
        _ctx_4096t = _ctx_4096t * jax.lax.rsqrt(jnp.mean(jnp.square(_ctx_4096t)) + 1e-12) * 0.953939
        ctx_4096 = -0.00010331 + 0.999899 * (_ctx_4096t + 0.3 * jax.random.normal(jax.random.fold_in(_rk, 611), (8, 375, 1024), jnp.float32))
        return (x, ctx_4096)
    x, ctx_4096 = _rec_inputs()

    def _L0_attn_setup():
        import jax, jax.numpy as jnp
        import numpy as np
        H = 1024
        D_IN = 2048
        N = 16
        K = 4
        R = 64
        EPS = 1e-06

        def rms_forward(x, eps=EPS):
            xf = x.astype(jnp.float32)
            var = jnp.mean(xf * xf, axis=-1, keepdims=True)
            return (xf * jax.lax.rsqrt(var + eps)).astype(x.dtype)
        key = jax.random.key(seed)
        ks = jax.random.split(key, 10)
        s = 0.02
        hidden_states = jax.random.normal(ks[0], (2, 256, H), dtype=jnp.float32)
        W_in = jax.random.normal(ks[1], (2 * D_IN, H), dtype=jnp.float32) * s
        conv_w = jax.random.normal(ks[2], (D_IN, K), dtype=jnp.float32) * 0.2
        conv_b = jax.random.normal(ks[3], (D_IN,), dtype=jnp.float32) * 0.02
        W_x = jax.random.normal(ks[4], (R + 2 * N, D_IN), dtype=jnp.float32) * s
        W_dt = jax.random.normal(ks[5], (D_IN, R), dtype=jnp.float32) * s
        b_dt = jax.random.normal(ks[6], (D_IN,), dtype=jnp.float32) * 0.02
        A_log = jnp.log(jnp.broadcast_to(jnp.arange(1, N + 1, dtype=jnp.float32)[None, :], (D_IN, N)))
        D = jnp.ones((D_IN,), dtype=jnp.float32)
        W_out = jax.random.normal(ks[7], (H, D_IN), dtype=jnp.float32) * s
        return {'hidden_states': hidden_states, 'W_in': W_in, 'conv_w': conv_w, 'conv_b': conv_b, 'W_x': W_x, 'W_dt': W_dt, 'b_dt': b_dt, 'A_log': A_log, 'D': D, 'W_out': W_out}
    _L0_attn_all = _L0_attn_setup()
    _L0_attn_in = {k: v for k, v in _L0_attn_all.items() if k in ('W_in', 'conv_w', 'conv_b', 'W_x', 'W_dt', 'b_dt', 'A_log', 'D', 'W_out')}
    del _L0_attn_all

    def _L0_xattn_setup():
        import jax, jax.numpy as jnp
        import numpy as np
        key = jax.random.key(seed)
        k1, k2 = jax.random.split(key)
        B, Lq, Lk, D = (16, 256, 512, 1024)
        query = jax.random.normal(k1, (B, Lq, D), dtype=jnp.float32)
        key_t = jax.random.normal(k2, (B, Lk, D), dtype=jnp.float32)
        return {'query': query, 'key': key_t}
    _L0_xattn_all = _L0_xattn_setup()
    _L0_xattn_in = {k: v for k, v in _L0_xattn_all.items() if k in ()}
    del _L0_xattn_all

    def _L0_ffn_setup():
        import jax, jax.numpy as jnp
        import numpy as np
        K_TOP = 8
        key = jax.random.key(seed)
        k1, k2, k3 = jax.random.split(key, 3)
        B, S, H, E = (4, 1024, 1024, 64)
        hidden_states = jax.random.normal(k1, (B, S, H), dtype=jnp.float32)
        router_weight = jax.random.normal(k2, (E, H), dtype=jnp.float32)
        router_bias = jnp.zeros((E,), dtype=jnp.float32)
        expert_bias = jax.random.normal(k3, (E, H), dtype=jnp.float32) * 0.1
        return {'hidden_states': hidden_states, 'router_weight': router_weight, 'router_bias': router_bias, 'expert_bias': expert_bias}
    _L0_ffn_all = _L0_ffn_setup()
    _L0_ffn_in = {k: v for k, v in _L0_ffn_all.items() if k in ('router_weight', 'router_bias', 'expert_bias')}
    del _L0_ffn_all
    return {'x': x, 'ctx_4096': ctx_4096, 'L0_attn_W_in': _L0_attn_in['W_in'], 'L0_attn_conv_w': _L0_attn_in['conv_w'], 'L0_attn_conv_b': _L0_attn_in['conv_b'], 'L0_attn_W_x': _L0_attn_in['W_x'], 'L0_attn_W_dt': _L0_attn_in['W_dt'], 'L0_attn_b_dt': _L0_attn_in['b_dt'], 'L0_attn_A_log': _L0_attn_in['A_log'], 'L0_attn_D': _L0_attn_in['D'], 'L0_attn_W_out': _L0_attn_in['W_out'], 'L0_ffn_router_weight': _L0_ffn_in['router_weight'], 'L0_ffn_router_bias': _L0_ffn_in['router_bias'], 'L0_ffn_expert_bias': _L0_ffn_in['expert_bias']}

def reference(x, ctx_4096, L0_attn_W_in, L0_attn_conv_w, L0_attn_conv_b, L0_attn_W_x, L0_attn_W_dt, L0_attn_b_dt, L0_attn_A_log, L0_attn_D, L0_attn_W_out, L0_ffn_router_weight, L0_ffn_router_bias, L0_ffn_expert_bias):
    import jax
    import jax.numpy as jnp

    def _L0_attn_ref(hidden_states, W_in, conv_w, conv_b, W_x, W_dt, b_dt, A_log, D, W_out):
        import jax, jax.numpy as jnp
        import numpy as np
        H = 1024
        D_IN = 2048
        N = 16
        K = 4
        R = 64
        EPS = 1e-06

        def rms_forward(x, eps=EPS):
            xf = x.astype(jnp.float32)
            var = jnp.mean(xf * xf, axis=-1, keepdims=True)
            return (xf * jax.lax.rsqrt(var + eps)).astype(x.dtype)
        b, L, _ = hidden_states.shape
        proj = hidden_states @ W_in.T
        x, gate = (proj[..., :D_IN], proj[..., D_IN:])
        xpad = jnp.pad(x, ((0, 0), (K - 1, 0), (0, 0)))
        xc = conv_b
        for j in range(K):
            xc = xc + conv_w[:, j] * xpad[:, j:j + L, :]
        x = jax.nn.silu(xc)
        ssm = x @ W_x.T
        ts, Bm, Cm = (ssm[..., :R], ssm[..., R:R + N], ssm[..., R + N:])
        ts = rms_forward(ts)
        Bm = rms_forward(Bm)
        Cm = rms_forward(Cm)
        dt = jax.nn.softplus(ts @ W_dt.T + b_dt)
        A = -jnp.exp(A_log.astype(jnp.float32))

        def step(state, inp):
            dt_t, B_t, C_t, u_t = inp
            dA = jnp.exp(dt_t[..., None] * A)
            state = state * dA + (dt_t * u_t)[..., None] * B_t[:, None, :]
            y = jnp.einsum('bdn,bn->bd', state, C_t)
            return (state, y)
        init = jnp.zeros((b, D_IN, N), dtype=jnp.float32)
        xs = (dt.transpose(1, 0, 2), Bm.transpose(1, 0, 2), Cm.transpose(1, 0, 2), x.transpose(1, 0, 2))
        _, ys = jax.lax.scan(step, init, xs)
        y = ys.transpose(1, 0, 2) + x * D
        y = y * jax.nn.silu(gate)
        return y @ W_out.T

    def _L0_xattn_ref(query, key):
        import jax, jax.numpy as jnp
        import numpy as np
        a = jnp.einsum('bqd,bkd->bqk', query, key)
        e = jax.nn.softmax(a, axis=-1)
        c = jnp.einsum('bqk,bkd->bqd', e, key)
        return c

    def _L0_ffn_ref(hidden_states, router_weight, router_bias, expert_bias):
        import jax, jax.numpy as jnp
        import numpy as np
        K_TOP = 8
        B, S, H = hidden_states.shape
        E = router_weight.shape[0]
        T = B * S
        flat = hidden_states.reshape(T, H)
        logits = jnp.einsum('th,eh->te', flat, router_weight) + router_bias
        scores = jax.nn.softmax(logits, axis=-1)
        topk_w, topk_idx = jax.lax.top_k(scores, K_TOP)
        w_sum = topk_w.sum(axis=-1, keepdims=True)
        w_dense = jnp.zeros((T, E), dtype=scores.dtype).at[jnp.arange(T)[:, None], topk_idx].add(topk_w)
        bias_mix = jnp.einsum('te,eh->th', w_dense, expert_bias)
        out = flat * w_sum + bias_mix
        return out.reshape(B, S, H)
    x = x + _L0_attn_ref(_layernorm(x, axis=-1), L0_attn_W_in, L0_attn_conv_w, L0_attn_conv_b, L0_attn_W_x, L0_attn_W_dt, L0_attn_b_dt, L0_attn_A_log, L0_attn_D, L0_attn_W_out)
    x = x + _L0_xattn_ref(_layernorm(x, axis=-1), ctx_4096)
    x = x + _L0_ffn_ref(_layernorm(x, axis=-1), L0_ffn_router_weight, L0_ffn_router_bias, L0_ffn_expert_bias)
    return x

_drawn_inputs = setup_inputs


def setup_inputs(seed=0):
    import zlib

    import numpy as np

    out = dict(_drawn_inputs(seed))
    spreads = {'L0_attn_D': (1.0, 0.55), 'L0_ffn_router_bias': (0.0, 0.8)}
    factors = {'L0_attn_b_dt': 8.0}
    for name, (base, spread) in spreads.items():
        noise = np.random.default_rng([zlib.crc32(name.encode()), seed]).standard_normal(out[name].shape)
        drawn = base * np.exp(spread * noise) if base else spread * noise
        out[name] = jnp.asarray(drawn.astype(out[name].dtype))
    for name, factor in factors.items():
        out[name] = (out[name] * factor).astype(out[name].dtype)
    return out
```

```python
import concourse.bass as bass
from concourse import mybir
from contextlib import ExitStack

F32 = mybir.dt.float32
ALU = mybir.AluOpType
ACT = mybir.ActivationFunctionType
AX = mybir.AxisListType

B, L, H = 8, 112, 1024
DI, NS, R, KC = 2048, 16, 64, 4
SK = 375
E = 64
P = 128
G, GB = 2, 4
GT = GB * L
NI, NK = DI // P, H // P
NQ, QI = 4, 4
QD = QI * P
SSM = R + 2 * NS
SC = SK // 3
LN_EPS, RMS_EPS = 1e-5, 1e-6
LAG = 3
STEPS = NS * GB
LOG_EXP = "natural_log_exp_and_others"

W_ON_DVE = (3,)
C_ON_DVE = (3,)
W_ON_ACT = tuple(b for b in range(GB) if b not in W_ON_DVE)
C_ON_POOL = tuple(b for b in range(GB) if b not in C_ON_DVE)


def misc_uses():
    order = []
    for g in range(G):
        order += [("ssm", g), ("ssm_tokens", g), ("ssm_back", g)]
        for dq in range(NQ):
            if dq == 0:
                order += [("dt", g, 0, i) for i in range(QI)] + [("du", g, 0, b) for b in range(GB)]
            else:
                order += [("y", g, dq - 1, i) for i in range(QI)]
            if dq < NQ - 1:
                order += [("dt", g, dq + 1, i) for i in range(QI)] + [("du", g, dq + 1, b) for b in range(GB)]
        order += [("y", g, NQ - 1, i) for i in range(QI)]
    return {what: n for n, what in enumerate(order)}


MISC = misc_uses()


def acc_use(it, j):
    if it < NQ:
        return 8 * it + j
    return 8 * NQ + 6 * (it - NQ) + (j // 2 if j < 4 else j - 2)


def weight_use(it, j):
    return 2 * (it // NQ + 1) + 8 * it + j


def of_batches(step, batches):
    return step // GB * len(batches) + sum(b in batches for b in range(step % GB))


def decoder_layer(nc, x, ctx, ctx_t, w_in, w_out, w_x, w_dt, conv_w, conv_b, b_dt, a_log, d_skip,
                  w_router, b_router, e_bias, out):
    c_rows = nc.dram_tensor("c_rows", (G, NS, GT), F32, kind="Internal").ap()
    with ExitStack() as stack:
        def sb(name, shape):
            return stack.enter_context(nc.sbuf_tensor(name, shape, F32))

        def bank(name):
            return stack.enter_context(nc.psum_tensor(name, [P, 512], F32))

        def sem(name):
            return stack.enter_context(nc.semaphore(name))

        xs = sb("xs", [P, NI, B * L])
        xnT = sb("xnT", [P, NK, B * L])
        c_region = sb("c_region", [P, NS * GT])
        arena = sb("arena", [P, 4 * QI * GT])
        dtu_region = sb("dtu_region", [P, 2 * GB * QD])
        gate = sb("gate", [P, QI, GT])
        tmp = sb("tmp", [P, GB * QD])
        w_tok = sb("w_tok", [L, 4, QD])
        h = sb("h", [P, 4, QI, L])
        wr = sb("wr", [P, 2, NK * P])
        wdt = sb("wdt", [R, 2, QD])
        ident = sb("ident", [P, P])
        ssm_t = sb("ssm_t", [SSM, GT])
        nrm = sb("nrm", [L, G, GB, SSM])
        ms = sb("ms", [L, 3, GB])
        stats = sb("stats", [L, 2, 16])
        cw = sb("cw", [P, NI, KC])
        cb = sb("cb", [P, NI])
        bdt = sb("bdt", [P, NI])
        dsk = sb("dsk", [P, NI])
        a_neg = sb("a_neg", [P, NI, NS])
        rb = sb("rb", [1, E])
        ones = sb("ones", [1, L])
        sm = sb("sm", [L, 2, 32])
        eps_ln = sb("eps_ln", [P, 1])

        c_bc = c_region[:, :].rearrange("p (n t) -> p n t", n=NS)
        w_first = arena[:, 0:4 * NK * P].rearrange("p (s n) -> p s n", s=4)
        dt = arena[:, 0:2 * QI * GT].rearrange("p (s i t) -> p s i t", s=2, i=QI)
        decay = arena[:, 2 * QI * GT:].rearrange("p (s b i t) -> p s b i t", s=2, b=GB, i=QI)
        dtu = dtu_region[0:L, :].rearrange("p (s b d) -> p s b d", s=2, b=GB)
        xt = dtu_region[0:L, 0:2 * H].rearrange("p (s c) -> p s c", s=2)
        xn = dtu_region[0:L, 2 * H:4 * H].rearrange("p (s c) -> p s c", s=2)
        tok = w_tok[:, 0, 0:GB * SSM].rearrange("p (b d) -> p b d", b=GB)
        tok_sq = w_tok[:, 1, 0:GB * SSM].rearrange("p (b d) -> p b d", b=GB)
        y_t = tmp[0:L, :].rearrange("p (b d) -> p b d", b=GB)
        lin = tmp[:, 0:QI * GT].rearrange("p (i t) -> p i t", i=QI)
        kT = c_region[:, 0:2 * NK * SK].rearrange("p (s k c) -> p s k c", s=2, k=NK)
        kv = arena[0:SC, 0:2 * 3 * H].rearrange("p (s c n) -> p s c n", s=2, c=3)
        o_b = gate[:, :, :].rearrange("p i t -> p (i t)").rearrange("p (s k t) -> p s k t", s=2, k=NK)
        q_b = tmp[:, 0:2 * NK * L].rearrange("p (s k t) -> p s k t", s=2, k=NK)
        res = w_tok[:, :, :].rearrange("p (s a) d -> p s (a d)", s=2)
        h_flat = h[:, :, :, :].rearrange("p s i t -> p (s i t)")
        e_b = h_flat[0:L, 0:2 * SK].rearrange("p (s c) -> p s c", s=2)
        eT = h_flat[0:SC, 752:752 + 6 * L].rearrange("p (s c t) -> p s c t", s=2, c=3)
        eb = wdt[:, :, :].rearrange("p s d -> p (s d)")
        rw = c_region[:, 2 * NK * SK:2 * NK * SK + NK * E].rearrange("p (k e) -> p k e", k=NK)
        r_b = nrm[:, :, :, :].rearrange("p g b d -> p (g b d)")
        rT = ssm_t[0:E, 0:2 * L].rearrange("p (s t) -> p s t", s=2)

        Y = [bank(f"y{b}") for b in range(GB)]
        WB = [bank(f"w{s}") for s in range(2)]
        ACC = bank("acc")
        MB = bank("misc")

        const_in = sem("const_in")
        ident_ok = sem("ident_ok")
        x_in = [sem(f"x_in{s}") for s in range(2)]
        a_exp = sem("a_exp")
        a_ready = sem("a_ready")
        ln_chain = sem("ln_chain")
        mv_ready = sem("mv_ready")
        lv_ready = sem("lv_ready")
        rstd_ready = sem("rstd_ready")
        xn_ready = sem("xn_ready")
        lnT_full = sem("lnT_full")
        lnT_used = sem("lnT_used")
        wf_in = [sem(f"wf_in{s}") for s in range(4)]
        xf_full = sem("xf_full")
        xf_started = sem("xf_started")
        xf_used = sem("xf_used")
        conv_chain = sem("conv_chain")
        x_silu = sem("x_silu")
        w_in_sem = [sem(f"w_in{s}") for s in range(2)]
        w_used = sem("w_used")
        wdt_in = [sem(f"wdt_in{s}") for s in range(2)]
        misc_full = sem("misc_full")
        misc_used = sem("misc_used")
        acc_full = sem("acc_full")
        acc_used = sem("acc_used")
        conv_started = sem("conv_started")
        ssm_chain = sem("ssm_chain")
        sq_ready = sem("sq_ready")
        ms_ready = sem("ms_ready")
        ms_log = sem("ms_log")
        rs_ready = sem("rs_ready")
        nrm_ready = sem("nrm_ready")
        c_stored = sem("c_stored")
        c_in = [sem(f"c_in{k}") for k in range(4)]
        abs_done = sem("abs_done")
        lin_done = sem("lin_done")
        soft_exp = sem("soft_exp")
        soft_done = sem("soft_done")
        dt_ready = sem("dt_ready")
        u_ready = sem("u_ready")
        dtu_ready = sem("dtu_ready")
        zero_cols = sem("zero_cols")
        decay_ready = sem("decay_ready")
        w_act = sem("w_act")
        w_dve = sem("w_dve")
        wT_done = sem("wT_done")
        scan_done = sem("scan_done")
        hc_pool = sem("hc_pool")
        hc_dve = sem("hc_dve")
        yT_done = sem("yT_done")
        y_out = sem("y_out")
        gate_raw = sem("gate_raw")
        gate_silu = sem("gate_silu")
        y_skip = sem("y_skip")
        y_ready = sem("y_ready")
        op_full = sem("op_full")
        op_used = sem("op_used")
        t_x = [sem(f"t_x{s}") for s in range(2)]
        t_kT = [sem(f"t_kT{s}") for s in range(2)]
        t_kv = [sem(f"t_kv{s}") for s in range(2)]
        tn = {n: sem("tail_" + n) for n in (
            "o_b", "oT", "x1", "chain", "mv1", "lv1", "rs1", "xn1", "xT1", "q1", "sc", "mx", "e", "rsum", "eTp",
            "eT", "pv", "x2", "mv2", "lv2", "rs2", "xn2", "xT2", "q2", "lg", "lmx", "le", "wn", "wTp", "wT",
            "mix", "res1", "res2")}
        t_out = [sem(f"t_out{s}") for s in range(2)]

        block = stack.enter_context(nc.Block())

        @block.sync
        def _(sp):
            def load_x(b, s):
                sp.dma_start(xt[:, s, :], x[b, :, :]).then_inc(x_in[s], 16)

            def load_first(i, s):
                sp.dma_start(w_first[:, s, :], w_in[i, :, :]).then_inc(wf_in[s], 16)

            def load_weights(u, source):
                if u >= 2:
                    sp.wait_ge(w_used, u - 1)
                n = source.shape[1]
                sp.dma_start(wr[:, u % 2, 0:n], source).then_inc(w_in_sem[u % 2], 16)

            def load_wdt(it):
                if it >= 2:
                    sp.wait_ge(misc_full, MISC[("dt", (it - 2) // NQ, (it - 2) % NQ, QI - 1)] + 1)
                dq = it % NQ
                sp.dma_start(wdt[:, it % 2, :], w_dt[:, dq * QD:(dq + 1) * QD]).then_inc(wdt_in[it % 2], 16)

            load_x(0, 0)
            load_x(1, 1)
            for t, src in ((cw[:, :, :], conv_w), (cb[:, :], conv_b), (bdt[:, :], b_dt), (dsk[:, :], d_skip),
                           (a_neg[:, :, :], a_log), (rb[:, :], b_router)):
                sp.dma_start(t, src).then_inc(const_in, 16)
            for s in range(4):
                load_first(s, s)
            for s in range(2):
                sp.wait_ge(xn_ready, s + 1)
                load_x(2 + s, s)
            sp.wait_ge(xn_ready, 3)
            load_x(4, 0)
            for jj in range(4):
                if jj < 3:
                    sp.wait_ge(xn_ready, 4 + jj)
                    load_x(5 + jj, (5 + jj) % 2)
                    for s in range(4):
                        sp.wait_ge(xf_full, 4 * jj + s + 1)
                        load_first(4 * (jj + 1) + s, s)
            for g in range(G):
                for hf in range(2):
                    load_weights(weight_use(NQ * g, 0) - 2 + hf, w_x[hf, :, :])
                load_wdt(NQ * g)
                load_weights(weight_use(NQ * g, 0), w_in[NI * 0 + 0, :, :] if g == 0 else w_out[0, :, :])
                sp.wait_ge(misc_used, MISC[("ssm_back", g)] + 1)
                sp.dma_start(c_rows[g, :, :], ssm_t[R + NS:SSM, :]).then_inc(c_stored, 16)
                sp.wait_ge(c_stored, 16 * (g + 1))
                if g:
                    sp.wait_ge(yT_done, NQ * STEPS)
                for k in range(4):
                    part = c_rows[g, 4 * k:4 * k + 4, :].rearrange("n t -> (n t)")
                    sp.dma_start(c_region[:, 4 * k * GT:4 * (k + 1) * GT],
                                 part.partition_broadcast(P)).then_inc(c_in[k], 16)
                for dq in range(NQ):
                    it = NQ * g + dq
                    for j in range(8):
                        if j == 4 and dq < NQ - 1:
                            load_wdt(it + 1)
                        if dq == 0 and j == 0:
                            continue
                        if j >= 4:
                            source = w_in[NI + 4 * dq + j - 4, :, :]
                        elif g == 0:
                            source = w_in[4 * dq + j, :, :]
                        else:
                            source = w_out[4 * dq + j, :, :]
                        load_weights(weight_use(it, j), source)
            u0 = weight_use(2 * NQ - 1, 7) + 1
            for j in range(2 * NK):
                load_weights(u0 + j, w_out[j, :, :])
            sp.wait_ge(yT_done, 2 * NQ * STEPS)
            sp.dma_start(eb[0:E, :], e_bias).then_inc(const_in, 16)
            sp.dma_start(rw, w_router).then_inc(const_in, 16)

            def load_tail(b, s):
                sp.dma_start(kT[:, s, :, :], ctx_t[b, :, :, :]).then_inc(t_kT[s], 16)
                sp.dma_start(kv[:, s, :, :], ctx[b, :, :].rearrange("(c p) n -> p c n", p=SC)).then_inc(t_kv[s], 16)

            for s in range(2):
                load_tail(s, s)
            sp.wait_ge(y_ready, 2 * NQ * QI)
            for s in range(2):
                load_x(s, s)
            for b in range(B):
                s = b % 2
                sp.wait_ge(tn["res2"], b + 1)
                sp.dma_start(out[b, :, :], res[:, s, :]).then_inc(t_out[s], 16)
                if b + 2 < B:
                    load_tail(b + 2, s)
                    load_x(b + 2, s)
            for s in range(2):
                sp.wait_ge(t_out[s], 16 * B // 2)

        @block.gpsimd
        def _(pool):
            pool.memset(ident[:, :], 0.0).then_inc(ident_ok, 1)
            pool.memset(ones[:, :], 1.0)
            pool.memset(eps_ln[:, :], LN_EPS).then_inc(ident_ok, 1)
            pool.wait_ge(ident_ok, 2)
            pool.affine_select(out=ident[:, :], in_=ident[:, :], compare_op=ALU.not_equal, fill=1.0, base=0,
                               pattern=[[-1, P]], channel_multiplier=1).then_inc(ident_ok, 1)
            pool.wait_ge(xf_full, NI)
            pool.memset(decay[:, :, :, :, 0:1].rearrange("p s b i t -> p (s b i) t"), 0.0).then_inc(zero_cols, 1)

            def y_gate(g, dq, i):
                pool.wait_ge(y_skip, QI * (NQ * g + dq) + i + 1)
                pool.wait_ge(gate_silu, NQ * g + dq + 1)
                col = xs[:, QI * dq + i, g * GT:(g + 1) * GT]
                pool.tensor_tensor(col, col, gate[:, i, :], ALU.mult).then_inc(y_ready, 1)

            for g in range(G):
                for dq in range(NQ):
                    it = NQ * g + dq
                    for n in range(NS):
                        if dq == 0 and n % 4 == 0:
                            pool.wait_ge(c_in[n // 4], 16 * (g + 1))
                        for b in range(GB):
                            step = it * STEPS + n * GB + b
                            if b == 2 and dq > 0 and 2 <= n < 2 + QI:
                                y_gate(g, dq - 1, n - 2)
                            if b not in C_ON_POOL:
                                continue
                            pool.wait_ge(scan_done, step + 1)
                            c_n = c_bc[:, n, b * L:(b + 1) * L].unsqueeze(1).to_broadcast([P, QI, L])
                            pool.tensor_tensor(h[:, b, :, :], h[:, b, :, :], c_n, ALU.mult).then_inc(hc_pool, 1)
                for i in range(QI):
                    y_gate(g, NQ - 1, i)

        @block.scalar
        def _(act):
            def norm_scale(s, count, mv, lv, rs):
                act.wait_ge(mv, count)
                act.activation(stats[:, s, 14:15], stats[:, s, 13:14], ACT.Ln, bias=eps_ln[0:L, :]).then_inc(lv, 1)
                act.wait_ge(lv, count)
                act.activation(stats[:, s, 15:16], stats[:, s, 14:15], ACT.Exp, scale=-0.5).then_inc(rs, 1)

            def conv_start(psum, i, g, full, count, started):
                act.wait_ge(full, count)
                act.activation(xs[:, i, g * GT:(g + 1) * GT], psum[:, 0:GT], ACT.Identity,
                               bias=cb[:, i:i + 1], scale=cw[:, i, KC - 1:KC]).then_inc(started, 1)

            act.preload_act_table_set(LOG_EXP)
            act.wait_ge(ident_ok, 3)
            act.wait_ge(const_in, 16 * 6)
            act.activation(a_neg[:, :, :], a_neg[:, :, :], ACT.Exp).then_inc(a_exp, 1)
            for b in range(GB):
                norm_scale(b % 2, b + 1, mv_ready, lv_ready, rstd_ready)
                for half in range(2):
                    act.wait_ge(lnT_full, 2 * b + half + 1)
                    act.copy(xnT[:, 4 * half:4 * half + 4, b * L:(b + 1) * L],
                             Y[2 + half][:, 0:4 * L].rearrange("p (k t) -> p k t", k=4)).then_inc(lnT_used, 1)
            for jj in range(4):
                b = GB + jj
                norm_scale(b % 2, b + 1, mv_ready, lv_ready, rstd_ready)
                for j in range(4):
                    conv_start(Y[j % 2], 4 * jj + j, 0, xf_full, 4 * jj + j + 1, xf_started)
                for half in range(2):
                    act.wait_ge(lnT_full, 2 * b + half + 1)
                    act.copy(xnT[:, 4 * half:4 * half + 4, b * L:(b + 1) * L],
                             Y[2 + half][:, 0:4 * L].rearrange("p (k t) -> p k t", k=4)).then_inc(lnT_used, 1)
            act.wait_ge(conv_chain, 3 * NI)
            for dq in range(NQ):
                part = xs[:, QI * dq:QI * (dq + 1), 0:GT]
                act.activation(part, part, ACT.Silu).then_inc(x_silu, 1)
            act.preload_act_table_set(LOG_EXP)

            def ssm_norm(g):
                act.wait_ge(misc_full, MISC[("ssm", g)] + 1)
                act.copy(ssm_t[:, :], MB[0:SSM, 0:GT]).then_inc(misc_used, 1)
                act.wait_ge(ssm_chain, 7 * g + 1)
                act.activation(tok_sq[:, :, :], tok[:, :, :], ACT.Square).then_inc(sq_ready, 1)
                act.wait_ge(ms_ready, g + 1)
                act.activation(ms[:, :, :], ms[:, :, :], ACT.Ln).then_inc(ms_log, 1)
                act.wait_ge(ms_log, g + 1)
                act.activation(ms[:, :, :], ms[:, :, :], ACT.Exp, scale=-0.5).then_inc(rs_ready, 1)
                act.wait_ge(misc_full, MISC[("ssm_back", g)] + 1)
                if g:
                    act.wait_ge(misc_full, MISC[("dt", 0, NQ - 1, QI - 1)] + 1)
                act.copy(ssm_t[:, :], MB[0:SSM, 0:GT]).then_inc(misc_used, 1)

            def soft_abs(g, dq, i):
                it = NQ * g + dq
                act.wait_ge(misc_full, MISC[("dt", g, dq, i)] + 1)
                if it >= 2:
                    act.wait_ge(u_ready, it - 1)
                tile = QI * dq + i
                act.activation(dt[:, it % 2, i, :], MB[:, 0:GT], ACT.Abs, bias=bdt[:, tile:tile + 1])\
                   .then_inc(abs_done, 1)

            def soft_log(it):
                d = dt[:, it % 2, :, :]
                act.wait_ge(abs_done, QI * (it + 1))
                act.activation(d, d, ACT.Exp, scale=-1.0).then_inc(soft_exp, 1)
                act.wait_ge(soft_exp, it + 1)
                act.activation(d, d, ACT.Ln, bias=1.0).then_inc(soft_done, 1)

            def decay_tile(it, n, i):
                state = it * NS + n
                if i == 0:
                    act.wait_ge(dt_ready, it + 1)
                    if state >= 2:
                        act.wait_ge(scan_done, GB * (state - 1))
                tile = QI * (it % NQ) + i
                a = act.activation(decay[:, state % 2, :, i, 1:L],
                                   dt[:, it % 2, i, :].rearrange("p (b t) -> p b t", b=GB)[:, :, 1:L],
                                   ACT.Exp, scale=a_neg[:, tile, n:n + 1])
                if i == QI - 1:
                    a.then_inc(decay_ready, 1)

            def silus(g, dq):
                it = NQ * g + dq
                act.wait_ge(gate_raw, QI * (it + 1))
                act.activation(gate[:, :, :], gate[:, :, :], ACT.Silu).then_inc(gate_silu, 1)
                if g == 0:
                    act.wait_ge(conv_chain, 3 * (NI + QI * (dq + 1)))
                    part = xs[:, QI * dq:QI * (dq + 1), GT:2 * GT]
                    act.activation(part, part, ACT.Silu).then_inc(x_silu, 1)
                act.preload_act_table_set(LOG_EXP)

            for g in range(G):
                ssm_norm(g)
                for i in range(QI):
                    soft_abs(g, 0, i)
                soft_log(NQ * g)
                if g == 0:
                    act.wait_ge(zero_cols, 1)
                    act.wait_ge(a_ready, 1)
                for dq in range(NQ):
                    it = NQ * g + dq
                    if dq == 0:
                        for i in range(QI):
                            decay_tile(it, 0, i)
                    for n in range(NS):
                        for b in range(GB):
                            step = it * STEPS + n * GB + b
                            if b in W_ON_ACT:
                                if n == 0:
                                    act.wait_ge(dtu_ready, GB * it + b + 1)
                                if step >= 4:
                                    act.wait_ge(wT_done, step - 3)
                                act.activation(w_tok[:, b, :], dtu[:, it % 2, b, :], ACT.Copy,
                                               scale=nrm[:, g, b, R + n:R + n + 1]).then_inc(w_act, 1)
                            if n < NS - 1:
                                decay_tile(it, n + 1, b)
                            elif dq < NQ - 1:
                                decay_tile(it + 1, 0, b)
                            if b == 0 and g == 0 and n in (2, 4, 6, 8):
                                j = n // 2 - 1
                                conv_start(ACC, QI * dq + j, 1, acc_full, acc_use(it, j) + 1, conv_started)
                            if b == 2 and dq < NQ - 1:
                                if 5 <= n < 5 + QI:
                                    soft_abs(g, dq + 1, n - 5)
                                if n == 9:
                                    soft_log(it + 1)
                        if n == 0 and dq > 0:
                            silus(g, dq - 1)
                silus(g, NQ - 1)

            for pair in range(B // 2):
                slots = [(s, 2 * pair + s + 1) for s in range(2)]
                for s, c in slots:
                    norm_scale(s, c, tn["mv1"], tn["lv1"], tn["rs1"])
                for s, c in slots:
                    for half in range(2):
                        act.wait_ge(tn["xT1"], 2 * (c - 1) + half + 1)
                        act.copy(q_b[:, s, 4 * half:4 * half + 4, :],
                                 (WB[0], WB[1], ACC, MB)[2 * s + half][:, 0:4 * L].rearrange("p (k t) -> p k t", k=4))\
                           .then_inc(tn["q1"], 1)
                for s, c in slots:
                    act.wait_ge(tn["mx"], c)
                    act.activation(e_b[:, s, :], Y[2 * s][0:L, 0:SK], ACT.Exp, bias=sm[:, s, 0:1],
                                   accum_out=sm[:, s, 1:2]).then_inc(tn["e"], 1)
                for s, c in slots:
                    act.wait_ge(tn["eTp"], c)
                    act.copy(eT[:, s, :, :], Y[2 * s + 1][0:SC, 0:3 * L].rearrange("p (c t) -> p c t", c=3))\
                       .then_inc(tn["eT"], 1)
                for s, c in slots:
                    norm_scale(s, c, tn["mv2"], tn["lv2"], tn["rs2"])
                for s, c in slots:
                    for half in range(2):
                        act.wait_ge(tn["xT2"], 2 * (c - 1) + half + 1)
                        act.copy(q_b[:, s, 4 * half:4 * half + 4, :],
                                 Y[2 * s + half][:, 0:4 * L].rearrange("p (k t) -> p k t", k=4)).then_inc(tn["q2"], 1)
                for s, c in slots:
                    act.wait_ge(tn["lmx"], c)
                    act.activation(r_b[:, 192 * s:192 * s + E], (WB[0], ACC)[s][0:L, 0:E], ACT.Exp,
                                   bias=sm[:, s, 3:4], accum_out=sm[:, s, 4:5]).then_inc(tn["le"], 1)
                for s, c in slots:
                    act.wait_ge(tn["wTp"], c)
                    act.copy(rT[:, s, :], (WB[1], MB)[s][0:E, 0:L]).then_inc(tn["wT"], 1)

        @block.tensor
        def _(pe):
            def transpose(o, i, last=True, start=True):
                k = i.shape[0]
                return pe.matmul(o, lhsT=i, rhs=ident[0:k, 0:k], start=start, stop=last, is_transpose=True)

            def turn_rows(rows, s, banks, full, used, count):
                for half in range(2):
                    if used is not None and count >= 2:
                        pe.wait_ge(used, 2 * (count - 2) + half + 1)
                    for k in range(4):
                        last = transpose(banks[half][:, k * L:(k + 1) * L],
                                         rows[:, s, (4 * half + k) * P:(4 * half + k + 1) * P])
                    last.then_inc(full, 1)

            pe.wait_ge(ident_ok, 3)
            for b in range(GB):
                pe.wait_ge(xn_ready, b + 1)
                turn_rows(xn, b % 2, Y[2:4], lnT_full, lnT_used, b + 1)
            pe.wait_ge(lnT_used, 2 * GB)
            for jj in range(4):
                for j in range(4):
                    i = 4 * jj + j
                    pe.wait_ge(wf_in[j], 16 * (jj + 1))
                    if i >= 2:
                        pe.wait_ge(xf_used, i - 1)
                    for k in range(NK):
                        last = pe.matmul(Y[j % 2][:, 0:GT], lhsT=w_first[:, j, k * P:(k + 1) * P],
                                         rhs=xnT[:, k, 0:GT], start=(k == 0), stop=(k == NK - 1))
                    last.then_inc(xf_full, 1)
                b = GB + jj
                pe.wait_ge(xn_ready, b + 1)
                turn_rows(xn, b % 2, Y[2:4], lnT_full, lnT_used, b + 1)
            pe.wait_ge(lnT_used, 2 * B)

            def misc(what, used_before=True):
                m = MISC[what]
                if m:
                    pe.wait_ge(misc_used, m)

            def ssm_steps(g):
                misc(("ssm", g))
                u = weight_use(NQ * g, 0) - 2
                for i in range(NI):
                    if i % 8 == 0:
                        pe.wait_ge(w_in_sem[(u + i // 8) % 2], 16 * ((u + i // 8) // 2 + 1))
                    if i % QI == 0:
                        pe.wait_ge(x_silu, NQ * g + i // QI + 1)
                    last = pe.matmul(MB[0:SSM, 0:GT], lhsT=wr[:, (u + i // 8) % 2, (i % 8) * SSM:(i % 8 + 1) * SSM],
                                     rhs=xs[:, i, g * GT:(g + 1) * GT], start=(i == 0), stop=(i == NI - 1))
                    if i == 7:
                        last.then_inc(w_used, 1)
                last.then_inc(misc_full, 1)
                pe.wait_ge(misc_full, MISC[("ssm", g)] + 1)
                pe.sem_inc(w_used, 1)
                misc(("ssm_tokens", g))
                for b in range(GB):
                    last = transpose(MB[0:L, b * SSM:(b + 1) * SSM], ssm_t[:, b * L:(b + 1) * L])
                last.then_inc(misc_full, 1)
                misc(("ssm_back", g))
                pe.wait_ge(nrm_ready, g + 1)
                for b in range(GB):
                    last = transpose(MB[0:SSM, b * L:(b + 1) * L], nrm[:, g, b, :])
                last.then_inc(misc_full, 1)

            def dt_tile(g, dq, i):
                it = NQ * g + dq
                misc(("dt", g, dq, i))
                pe.wait_ge(wdt_in[it % 2], 16 * (it // 2 + 1))
                pe.matmul(MB[:, 0:GT], lhsT=wdt[:, it % 2, i * P:(i + 1) * P], rhs=ssm_t[0:R, :],
                          start=True, stop=True).then_inc(misc_full, 1)

            def du_batch(g, dq, b):
                misc(("du", g, dq, b))
                pe.wait_ge(u_ready, NQ * g + dq + 1)
                for i in range(QI):
                    last = transpose(MB[0:L, i * P:(i + 1) * P], lin[:, i, b * L:(b + 1) * L])
                last.then_inc(misc_full, 1)

            def y_tile(g, dq, i):
                misc(("y", g, dq, i))
                pe.wait_ge(y_out, GB * (NQ * g + dq + 1))
                for b in range(GB):
                    last = transpose(MB[:, b * L:(b + 1) * L], y_t[:, b, i * P:(i + 1) * P])
                last.then_inc(misc_full, 1)

            def sum_states(step):
                it, n, b = step // STEPS, step % STEPS // GB, step % GB
                if b in C_ON_POOL:
                    pe.wait_ge(hc_pool, of_batches(step + 1, C_ON_POOL))
                else:
                    pe.wait_ge(hc_dve, of_batches(step + 1, C_ON_DVE))
                if n == 0 and it:
                    pe.wait_ge(y_out, GB * (it - 1) + b + 1)
                for i in range(QI):
                    last = transpose(Y[b][0:L, i * P:(i + 1) * P], h[:, b, i, :],
                                     last=(n == NS - 1 and i == QI - 1), start=(n == 0 and i == 0))
                last.then_inc(yT_done, 1)

            def projection(it, j, k):
                g, dq = it // NQ, it % NQ
                u = weight_use(it, j)
                opens = not (g and j in (1, 3))
                if k == 0:
                    pe.wait_ge(w_in_sem[u % 2], 16 * (u // 2 + 1))
                    if opens and acc_use(it, j):
                        pe.wait_ge(acc_used, acc_use(it, j))
                w = wr[:, u % 2, k * P:(k + 1) * P]
                if j >= 4:
                    rhs = xnT[:, k, g * GT:(g + 1) * GT]
                elif g == 0:
                    rhs = xnT[:, k, GT:2 * GT]
                else:
                    rhs = xs[:, 8 * (j % 2) + k, 0:GT]
                closes = k == NK - 1 and not (g and j in (0, 2))
                last = pe.matmul(ACC[:, 0:GT], lhsT=w, rhs=rhs, start=(k == 0 and opens), stop=closes)
                if k == NK - 1:
                    last.then_inc(w_used, 1)
                    if closes:
                        pe.wait_ge(w_used, u + 1)
                        pe.sem_inc(acc_full, 1)

            for g in range(G):
                ssm_steps(g)
                for i in range(QI):
                    dt_tile(g, 0, i)
                for b in range(GB):
                    du_batch(g, 0, b)
                if g == 1:
                    pe.wait_ge(y_ready, NQ * QI)
                for dq in range(NQ):
                    it = NQ * g + dq
                    for n in range(NS):
                        for b in range(GB):
                            step = it * STEPS + n * GB + b
                            if b in W_ON_ACT:
                                pe.wait_ge(w_act, of_batches(step + 1, W_ON_ACT))
                            else:
                                pe.wait_ge(w_dve, of_batches(step + 1, W_ON_DVE))
                            if step >= 2:
                                pe.wait_ge(scan_done, step - 1)
                            for i in range(QI):
                                last = transpose(WB[step % 2][:, i * L:(i + 1) * L], w_tok[:, b, i * P:(i + 1) * P])
                            last.then_inc(wT_done, 1)
                            if step - LAG >= NQ * g * STEPS:
                                sum_states(step - LAG)
                            j, q = n // 2, n % 2 * GB + b
                            if q:
                                projection(it, j, q - 1)
                            if q == 7:
                                projection(it, j, 7)
                            if b == 1 and dq > 0 and 1 <= n < 1 + QI:
                                y_tile(g, dq - 1, n - 1)
                            if b == 1 and dq < NQ - 1:
                                if 5 <= n < 5 + QI:
                                    dt_tile(g, dq + 1, n - 5)
                                if 11 <= n < 11 + GB:
                                    du_batch(g, dq + 1, n - 11)
                for step in range(NQ * (g + 1) * STEPS - LAG, NQ * (g + 1) * STEPS):
                    sum_states(step)
                for i in range(QI):
                    y_tile(g, NQ - 1, i)
            u = weight_use(2 * NQ - 1, 7) + 1
            pe.wait_ge(y_ready, 2 * NQ * QI)
            for ho in range(NK):
                if ho >= 2:
                    pe.wait_ge(op_used, ho - 1)
                for hf in range(2):
                    uu = u + 2 * ho + hf
                    pe.wait_ge(w_in_sem[uu % 2], 16 * (uu // 2 + 1))
                    for k in range(8):
                        last = pe.matmul(Y[ho % 2][:, 0:GT], lhsT=wr[:, uu % 2, k * P:(k + 1) * P],
                                         rhs=xs[:, 8 * hf + k, GT:2 * GT], start=(hf == 0 and k == 0),
                                         stop=(hf == 1 and k == 7))
                    last.then_inc(w_used, 1)
                pe.wait_ge(w_used, uu + 1)
                pe.sem_inc(op_full, 1)

            pe.wait_ge(op_used, NK)
            pe.wait_ge(const_in, 16 * 8)
            for pair in range(B // 2):
                slots = [(s, 2 * pair + s + 1) for s in range(2)]
                for s, c in slots:
                    pe.wait_ge(tn["o_b"], c)
                    if pair:
                        pe.wait_ge(tn["res2"], c - 2)
                    for half in range(2):
                        for k in range(4):
                            last = transpose(Y[2 * s + half][0:L, k * P:(k + 1) * P], o_b[:, s, 4 * half + k, :])
                    last.then_inc(tn["oT"], 1)
                for s, c in slots:
                    pe.wait_ge(tn["xn1"], c)
                    turn_rows(xn, s, ((WB[0], WB[1]), (ACC, MB))[s], tn["xT1"], None, 0)
                for s, c in slots:
                    pe.wait_ge(tn["q1"], 2 * c)
                    pe.wait_ge(t_kT[s], 16 * (pair + 1))
                    for k in range(NK):
                        last = pe.matmul(Y[2 * s][0:L, 0:SK], lhsT=q_b[:, s, k, :], rhs=kT[:, s, k, :],
                                         start=(k == 0), stop=(k == NK - 1))
                    last.then_inc(tn["sc"], 1)
                for s, c in slots:
                    pe.wait_ge(tn["e"], c)
                    for k in range(3):
                        last = transpose(Y[2 * s + 1][0:SC, k * L:(k + 1) * L], e_b[:, s, k * SC:(k + 1) * SC])
                    last.then_inc(tn["eTp"], 1)
                for s, c in slots:
                    pe.wait_ge(tn["eT"], c)
                    pe.wait_ge(t_kv[s], 16 * (pair + 1))
                    for half in range(2):
                        for k in range(3):
                            last = pe.matmul(((WB[0], WB[1]), (ACC, MB))[s][half][0:L, :], lhsT=eT[:, s, k, :],
                                             rhs=kv[:, s, k, half * 512:(half + 1) * 512], start=(k == 0), stop=(k == 2))
                    last.then_inc(tn["pv"], 1)
                for s, c in slots:
                    pe.wait_ge(tn["xn2"], c)
                    turn_rows(xn, s, Y[2 * s:2 * s + 2], tn["xT2"], None, 0)
                for s, c in slots:
                    pe.wait_ge(tn["q2"], 2 * c)
                    lg = (WB[0], ACC)[s][0:L, 0:E]
                    for k in range(NK):
                        pe.matmul(lg, lhsT=q_b[:, s, k, :], rhs=rw[:, k, :], start=(k == 0), stop=False)
                    pe.matmul(lg, lhsT=ones[:, :], rhs=rb[:, :], start=False, stop=True).then_inc(tn["lg"], 1)
                for s, c in slots:
                    pe.wait_ge(tn["wn"], c)
                    transpose((WB[1], MB)[s][0:E, 0:L], r_b[:, 192 * s + 128:192 * s + 192]).then_inc(tn["wTp"], 1)
                for s, c in slots:
                    pe.wait_ge(tn["wT"], c)
                    for half in range(2):
                        last = pe.matmul(Y[2 * s + half][0:L, :], lhsT=rT[:, s, :],
                                         rhs=eb[0:E, half * 512:(half + 1) * 512], start=True, stop=True)
                    last.then_inc(tn["mix"], 1)

        @block.vector
        def _(dve):
            def link(ins, chain, count):
                count[0] += 1
                ins.then_inc(chain, 1)
                dve.wait_ge(chain, count[0])

            ln_count = [0]
            conv_count = [0]
            tail_count = [0]

            def norm_stats(s, ready, chain, count):
                link(dve.bn_stats(stats[:, s, 0:6], xt[:, s, 0:512]), chain, count)
                link(dve.bn_stats(stats[:, s, 6:12], xt[:, s, 512:1024]), chain, count)
                dve.bn_aggr(stats[:, s, 12:14], stats[:, s, 0:12]).then_inc(ready, 1)

            def norm_apply(s, count, rs, ready):
                dve.wait_ge(rs, count)
                dve.tensor_scalar(xn[:, s, :], xt[:, s, :], stats[:, s, 12:13], stats[:, s, 15:16],
                                  ALU.subtract, ALU.mult).then_inc(ready, 1)

            def norm_row(b):
                s = b % 2
                dve.wait_ge(x_in[s], 16 * (b // 2 + 1))
                norm_stats(s, mv_ready, ln_chain, ln_count)
                if b >= 2:
                    dve.wait_ge(lnT_full, 2 * (b - 1))
                norm_apply(s, b + 1, rstd_ready, xn_ready)

            def conv(psum, i, g, started, count, used):
                dve.wait_ge(started, count)
                col = xs[:, i, g * GT:(g + 1) * GT].rearrange("p (b t) -> p b t", b=GB)
                raw = psum[:, 0:GT].rearrange("p (b t) -> p b t", b=GB)
                for back in range(1, KC):
                    ins = dve.scalar_tensor_tensor(col[:, :, back:L], raw[:, :, 0:L - back],
                                                   cw[:, i, KC - 1 - back:KC - back], col[:, :, back:L],
                                                   ALU.mult, ALU.add)
                    link(ins, conv_chain, conv_count)
                dve.sem_inc(used, 1)

            for b in range(GB):
                norm_row(b)
            dve.wait_ge(a_exp, 1)
            dve.tensor_scalar(a_neg[:, :, :], a_neg[:, :, :], -1.0, None, ALU.mult).then_inc(a_ready, 1)
            for jj in range(4):
                norm_row(GB + jj)
                for j in range(4):
                    conv(Y[j % 2], 4 * jj + j, 0, xf_started, 4 * jj + j + 1, xf_used)

            def ssm_norm(g):
                count = [7 * g]
                dve.wait_ge(misc_full, MISC[("ssm_tokens", g)] + 1)
                link(dve.tensor_copy(tok[:, :, :], MB[0:L, 0:GB * SSM].rearrange("p (b d) -> p b d", b=GB)),
                     ssm_chain, count)
                dve.sem_inc(misc_used, 1)
                dve.wait_ge(sq_ready, g + 1)
                parts = ((0, R), (R, R + NS), (R + NS, SSM))
                for k, (a, z) in enumerate(parts):
                    link(dve.reduce_sum(ms[:, k, :], tok_sq[:, :, a:z], AX.X), ssm_chain, count)
                link(dve.tensor_scalar(ms[:, 0, :], ms[:, 0, :], 1.0 / R, RMS_EPS, ALU.mult, ALU.add), ssm_chain, count)
                dve.tensor_scalar(ms[:, 1:3, :], ms[:, 1:3, :], 1.0 / NS, RMS_EPS, ALU.mult, ALU.add)\
                   .then_inc(ms_ready, 1)
                dve.wait_ge(rs_ready, g + 1)
                for k, (a, z) in enumerate(parts):
                    ins = dve.tensor_tensor(nrm[:, g, :, a:z], tok[:, :, a:z],
                                            ms[:, k, :].unsqueeze(2).to_broadcast([L, GB, z - a]), ALU.mult)
                    if k < 2:
                        link(ins, ssm_chain, count)
                ins.then_inc(nrm_ready, 1)

            def soft_lin(g, dq, i):
                it = NQ * g + dq
                tile = QI * dq + i
                dve.wait_ge(abs_done, QI * it + i + 1)
                dve.tensor_scalar(lin[:, i, :], MB[:, 0:GT], bdt[:, tile:tile + 1], 0.0, ALU.add, ALU.max)\
                   .then_inc(misc_used, 1)

            def soft_end(g, dq):
                it = NQ * g + dq
                d = dt[:, it % 2, :, :]
                dve.wait_ge(soft_done, it + 1)
                dve.wait_ge(misc_used, MISC[("dt", g, dq, QI - 1)] + 1)
                dve.tensor_tensor(d, d, lin, ALU.add).then_inc(dt_ready, 1)
                dve.wait_ge(dt_ready, it + 1)
                dve.tensor_tensor(lin, d, xs[:, QI * dq:QI * (dq + 1), g * GT:(g + 1) * GT], ALU.mult)\
                   .then_inc(u_ready, 1)

            def dtu_batch(g, dq, b):
                it = NQ * g + dq
                dve.wait_ge(misc_full, MISC[("du", g, dq, b)] + 1)
                dve.tensor_copy(dtu[:, it % 2, b, :], MB[0:L, :]).then_inc(misc_used, 1)
                dve.wait_ge(misc_used, MISC[("du", g, dq, b)] + 1)
                dve.sem_inc(dtu_ready, 1)

            def y_rows(it, b):
                dve.wait_ge(yT_done, (it + 1) * STEPS - GB + b + 1)
                dve.tensor_copy(y_t[:, b, :], Y[b][0:L, :]).then_inc(y_out, 1)

            def y_tile(g, dq, i):
                tile = QI * dq + i
                col = xs[:, tile, g * GT:(g + 1) * GT]
                dve.wait_ge(misc_full, MISC[("y", g, dq, i)] + 1)
                dve.scalar_tensor_tensor(col, col, dsk[:, tile:tile + 1], MB[:, 0:GT], ALU.mult, ALU.add)\
                   .then_inc(y_skip, 1)
                dve.wait_ge(y_skip, QI * (NQ * g + dq) + i + 1)
                dve.sem_inc(misc_used, 1)

            def projected(it, j):
                g, dq = it // NQ, it % NQ
                if g == 0 and j < 4:
                    conv(ACC, QI * dq + j, 1, conv_started, QI * dq + j + 1, acc_used)
                    return
                if g == 1 and j in (0, 2):
                    return
                dve.wait_ge(acc_full, acc_use(it, j) + 1)
                if j < 4:
                    dve.tensor_copy(xnT[:, 2 * dq + j // 2, 0:GT], ACC[:, 0:GT]).then_inc(acc_used, 1)
                    return
                if it:
                    dve.wait_ge(y_ready, QI * it)
                dve.tensor_copy(gate[:, j - 4, :], ACC[:, 0:GT]).then_inc(gate_raw, 1)
                dve.wait_ge(gate_raw, QI * it + j - 3)
                dve.sem_inc(acc_used, 1)

            def times_c(step):
                n, b = step % STEPS // GB, step % GB
                dve.wait_ge(scan_done, step + 1)
                c_n = c_bc[:, n, b * L:(b + 1) * L].unsqueeze(1).to_broadcast([P, QI, L])
                dve.tensor_tensor(h[:, b, :, :], h[:, b, :, :], c_n, ALU.mult).then_inc(hc_dve, 1)

            dve.wait_ge(zero_cols, 1)
            for g in range(G):
                ssm_norm(g)
                for i in range(QI):
                    soft_lin(g, 0, i)
                soft_end(g, 0)
                for b in range(GB):
                    dtu_batch(g, 0, b)
                for dq in range(NQ):
                    it = NQ * g + dq
                    for n in range(NS):
                        if dq == 0 and n % 4 == 0:
                            dve.wait_ge(c_in[n // 4], 16 * (g + 1))
                        for b in range(GB):
                            step = it * STEPS + n * GB + b
                            if b == 0:
                                for bb in W_ON_DVE:
                                    if n or it:
                                        dve.wait_ge(wT_done, step + bb - 3)
                                    dve.tensor_scalar(w_tok[:, bb, :], dtu[:, it % 2, bb, :],
                                                      nrm[:, g, bb, R + n:R + n + 1], None, ALU.mult).then_inc(w_dve, 1)
                            dve.wait_ge(wT_done, step + 1)
                            if b == 0:
                                dve.wait_ge(decay_ready, it * NS + n + 1)
                            if step >= 4 + NQ * g * STEPS:
                                dve.wait_ge(yT_done, step - 3)
                            dve.tensor_tensor_scan(h[:, b, :, :].rearrange("p i t -> p (i t)"),
                                                   decay[:, (it * NS + n) % 2, b, :, :].rearrange("p i t -> p (i t)"),
                                                   WB[step % 2][:, 0:QI * L], 0.0, ALU.mult, ALU.add)\
                               .then_inc(scan_done, 1)
                            if (b - 1) % GB in C_ON_DVE and step > NQ * g * STEPS:
                                times_c(step - 1)
                            if b == 0 and n % 2 == 0 and n:
                                projected(it, n // 2 - 1)
                            if b == 3 and dq > 0:
                                if n == 0:
                                    for bb in range(GB):
                                        y_rows(it - 1, bb)
                                if 1 <= n < 1 + QI:
                                    y_tile(g, dq - 1, n - 1)
                            if b == 3 and dq < NQ - 1:
                                if 5 <= n < 5 + QI:
                                    soft_lin(g, dq + 1, n - 5)
                                if n == 10:
                                    soft_end(g, dq + 1)
                                if 11 <= n < 11 + GB:
                                    dtu_batch(g, dq + 1, n - 11)
                    projected(it, 7)
                if GB - 1 in C_ON_DVE:
                    times_c(NQ * (g + 1) * STEPS - 1)
                for b in range(GB):
                    y_rows(NQ * (g + 1) - 1, b)
                for i in range(QI):
                    y_tile(g, NQ - 1, i)
            for ho in range(NK):
                dve.wait_ge(op_full, ho + 1)
                dve.tensor_copy(xnT[:, ho, GT:2 * GT], Y[ho % 2][:, 0:GT]).then_inc(op_used, 1)
            dve.wait_ge(op_used, NK)

            chain = tn["chain"]
            for pair in range(B // 2):
                slots = [(s, 2 * pair + s + 1) for s in range(2)]
                for s, c in slots:
                    b = c - 1
                    dve.tensor_copy(o_b[:, s, :, :], xnT[:, :, b * L:(b + 1) * L]).then_inc(tn["o_b"], 1)
                for s, c in slots:
                    dve.wait_ge(tn["oT"], c)
                    dve.wait_ge(x_in[s], 16 * (B // 2 + pair + 1))
                    for half in range(2):
                        part = xt[:, s, half * 512:(half + 1) * 512]
                        link(dve.tensor_tensor(part, part, Y[2 * s + half][0:L, :], ALU.add), chain, tail_count)
                    norm_stats(s, tn["mv1"], chain, tail_count)
                for s, c in slots:
                    norm_apply(s, c, tn["rs1"], tn["xn1"])
                for s, c in slots:
                    dve.wait_ge(tn["sc"], c)
                    dve.reduce_max(sm[:, s, 0:1], Y[2 * s][0:L, 0:SK], AX.X, negate=True).then_inc(tn["mx"], 1)
                for s, c in slots:
                    dve.wait_ge(tn["e"], c)
                    link(dve.reciprocal(sm[:, s, 2:3], sm[:, s, 1:2]), chain, tail_count)
                for s, c in slots:
                    dve.wait_ge(tn["pv"], c)
                    for half in range(2):
                        part = xt[:, s, half * 512:(half + 1) * 512]
                        link(dve.scalar_tensor_tensor(part, ((WB[0], WB[1]), (ACC, MB))[s][half][0:L, :],
                                                      sm[:, s, 2:3], part, ALU.mult, ALU.add), chain, tail_count)
                    norm_stats(s, tn["mv2"], chain, tail_count)
                for s, c in slots:
                    norm_apply(s, c, tn["rs2"], tn["xn2"])
                for s, c in slots:
                    dve.wait_ge(tn["lg"], c)
                    dve.reduce_max(sm[:, s, 3:4], (WB[0], ACC)[s][0:L, 0:E], AX.X, negate=True).then_inc(tn["lmx"], 1)
                for s, c in slots:
                    dve.wait_ge(tn["le"], c)
                    ex = r_b[:, 192 * s:192 * s + E]
                    rest = r_b[:, 192 * s + 64:192 * s + 128]
                    wn = r_b[:, 192 * s + 128:192 * s + 192]
                    link(dve.max(sm[:, s, 8:16], ex), chain, tail_count)
                    link(dve.match_replace(rest, sm[:, s, 8:16], ex, -1.0), chain, tail_count)
                    link(dve.scalar_tensor_tensor(wn, rest, 0.0, ex, ALU.max, ALU.subtract), chain, tail_count)
                    link(dve.reciprocal(sm[:, s, 5:6], sm[:, s, 4:5]), chain, tail_count)
                    link(dve.tensor_scalar(wn, wn, sm[:, s, 5:6], -1.0, ALU.mult, ALU.mult), chain, tail_count)
                    dve.sem_inc(tn["wn"], 1)
                    link(dve.reduce_sum(sm[:, s, 6:7], wn, AX.X), chain, tail_count)
                for s, c in slots:
                    if pair:
                        dve.wait_ge(t_out[s], 16 * pair)
                    dve.scalar_tensor_tensor(res[:, s, :], xn[:, s, :], sm[:, s, 6:7], xt[:, s, :],
                                             ALU.mult, ALU.add).then_inc(tn["res1"], 1)
                for s, c in slots:
                    dve.wait_ge(tn["mix"], c)
                    dve.wait_ge(tn["res1"], c)
                    for half in range(2):
                        part = res[:, s, half * 512:(half + 1) * 512]
                        ins = dve.tensor_tensor(part, part, Y[2 * s + half][0:L, :], ALU.add)
                        if half == 0:
                            link(ins, chain, tail_count)
                    ins.then_inc(tn["res2"], 1)


def kernel(**inputs):
    import numpy as np
    import concourse.bacc as bacc
    from concourse.bass_utils import run_bass_kernel_spmd

    a = {k: np.asarray(v) for k, v in inputs.items()}

    def tiles(w, rows):
        o, i = w.shape
        return w.reshape(o // rows, rows, i // 1024, 8, P).transpose(0, 2, 4, 3, 1).reshape(-1, P, 8 * rows)

    def channels(v):
        return v.reshape(NI, P, -1).transpose(1, 0, 2)

    arrays = {
        "x": a["x"],
        "ctx": a["ctx_4096"],
        "ctx_t": a["ctx_4096"].reshape(B, SK, NK, P).transpose(0, 3, 2, 1),
        "w_in": tiles(a["L0_attn_W_in"], P),
        "w_out": tiles(a["L0_attn_W_out"], P),
        "w_x": tiles(a["L0_attn_W_x"], SSM),
        "w_dt": a["L0_attn_W_dt"].T,
        "conv_w": channels(a["L0_attn_conv_w"]),
        "conv_b": channels(a["L0_attn_conv_b"])[:, :, 0],
        "b_dt": channels(a["L0_attn_b_dt"])[:, :, 0],
        "a_log": channels(a["L0_attn_A_log"]),
        "d_skip": channels(a["L0_attn_D"])[:, :, 0],
        "w_router": a["L0_ffn_router_weight"].reshape(E, NK, P).transpose(2, 1, 0),
        "b_router": a["L0_ffn_router_bias"].reshape(1, E),
        "e_bias": a["L0_ffn_expert_bias"],
    }
    arrays = {k: np.ascontiguousarray(v) for k, v in arrays.items()}
    nc = bacc.Bacc("TRN2", target_bir_lowering=False, num_devices=1)
    args = [nc.dram_tensor(k, v.shape, F32, kind="ExternalInput").ap() for k, v in arrays.items()]
    args.append(nc.dram_tensor("out", (B, L, H), F32, kind="ExternalOutput").ap())
    decoder_layer(nc, *args)
    r = run_bass_kernel_spmd(nc, [arrays], core_ids=[0])
    return r.results[0]["out"]
```

```python
import concourse.bass as bass
from concourse import mybir
from contextlib import ExitStack

F32 = mybir.dt.float32
F32R = mybir.dt.float32r
ALU = mybir.AluOpType
ACT = mybir.ActivationFunctionType
AX = mybir.AxisListType

B, L, H = 8, 112, 1024
DI, NS, R, KC = 2048, 16, 64, 4
SK = 375
E = 64
P = 128
G, GB = 2, 4
GT = GB * L
NI, NK = DI // P, H // P
NQ, QI = 4, 4
QD = QI * P
SSM = R + 2 * NS
SC = SK // 3
LN_EPS, RMS_EPS = 1e-5, 1e-6
LAG = 2
STEPS = NS * GB
LOG_EXP = "natural_log_exp_and_others"



def small_jobs():
    order = []
    for g in range(G):
        order += [("ssm", g), ("ssm_tokens", g), ("ssm_back", g)]
        for dq in range(NQ):
            if dq == 0:
                order += [("dt", g, 0, i) for i in range(QI)]
            else:
                order += [("y", g, dq - 1, i) for i in range(QI)]
            if dq < NQ - 1:
                order += [("dt", g, dq + 1, i) for i in range(QI)]
        order += [("y", g, NQ - 1, i) for i in range(QI)]
    return {what: n for n, what in enumerate(order)}


MISC = small_jobs()
Y_AT, DT_AT = 1, 5


def narrow(it, n):
    dq = it % NQ
    return (dq > 0 and Y_AT <= n < Y_AT + QI) or (dq < NQ - 1 and DT_AT <= n < DT_AT + QI)


def drive_bank(it, n, b):
    return 0 if b >= 2 and narrow(it, n) else b % 2


def last_in_bank(step):
    def bank_of(s):
        return drive_bank(s // STEPS, s % STEPS // GB, s % GB)
    return next((s for s in range(step - 1, max(step - 5, -1), -1) if bank_of(s) == bank_of(step)), None)


def job_bank(what):
    kind, i = what[0], what[-1]
    if kind == "y" and what[2] == NQ - 1:
        return i % 2
    if kind == "dt" and what[2] == 0:
        return (i + 1) % 2
    return {"ssm": 0, "ssm_tokens": 1, "ssm_back": 0}.get(kind, 1)


def acc_before(it, j):
    if it == 0 and j == 0:
        return None
    return (it - 1, 7) if j == 0 else (it, j - 1)


def weight_use(it, j):
    return 2 * (it // NQ + 1) + 8 * it + j


def tail_uses():
    order = []
    for g in range(G):
        for what, parts in (("out", 2), ("xT1", 2), ("scores", 1), ("eT", 1), ("pv", 2), ("xT2", 2), ("logits", 1),
                            ("wT", 1), ("mix", 2)):
            order += [(what, b, k) for b in range(GB * g, GB * (g + 1)) for k in range(parts)]
    return order


TAIL = tail_uses()
TAIL_AT = {what: n for n, what in enumerate(TAIL)}


def decoder_layer(nc, x, ctx, ctx_t, w_in, w_out, w_x, w_dt, conv_w, conv_b, b_dt, a_log, d_skip,
                  w_router, b_router, e_bias, out):
    c_rows = nc.dram_tensor("c_rows", (G, NS, GT), F32, kind="Internal").ap()
    with ExitStack() as stack:
        def sb(name, shape, dtype=F32):
            return stack.enter_context(nc.sbuf_tensor(name, shape, dtype))

        def bank(name):
            return stack.enter_context(nc.psum_tensor(name, [P, 512], F32))

        def sem(name):
            return stack.enter_context(nc.semaphore(name))

        xs = sb("xs", [P, G, NI, GT])
        xnT = sb("xnT", [P, NK, B * L])
        c_region = sb("c_region", [P, NS * GT])
        arena = sb("arena", [P, 4 * QI * GT])
        u_region = sb("u_region", [P, 2 * QI * GT])
        gate = sb("gate", [P, QI, GT])
        tmp = sb("tmp", [P, GB * QD])
        h = sb("h", [P, 4, QI, L])
        raw = sb("raw", [P, GT])
        wr = sb("wr", [P, 2, NK * P])
        wdt = sb("wdt", [R, 2, QD])
        ident = sb("ident", [P, P])
        ident_r = sb("ident_r", [SSM, SSM], F32R)
        ssm_t = sb("ssm_t", [SSM, GT])
        bc_hi = sb("bc_hi", [SSM, GT], F32R)
        bc_lo = sb("bc_lo", [SSM, GT], F32R)
        nrm = sb("nrm", [L, G, GB, SSM])
        ms = sb("ms", [L, 3, GB])
        stats = sb("stats", [L, GB, 16])
        sm = sb("sm", [L, GB, 16])
        cw = sb("cw", [P, NI, KC])
        cb = sb("cb", [P, NI])
        bdt = sb("bdt", [P, NI])
        dsk = sb("dsk", [P, NI])
        a_neg = sb("a_neg", [P, NI, NS])
        rb = sb("rb", [1, E])
        ones = sb("ones", [1, L])
        eps_ln = sb("eps_ln", [P, 1])

        c_bc = c_region[:, :].rearrange("p (n t) -> p n t", n=NS)
        w_first = arena[:, 0:4 * NK * P].rearrange("p (s n) -> p s n", s=4)
        dt = arena[:, 0:2 * QI * GT].rearrange("p (s i t) -> p s i t", s=2, i=QI)
        decay = arena[:, 2 * QI * GT:].rearrange("p (s b i t) -> p s b i t", s=2, b=GB, i=QI)
        u = u_region[:, :].rearrange("p (s i t) -> p s i t", s=2, i=QI)
        xt0 = [c_region[0:L, s * H:(s + 1) * H] for s in range(2)]
        xn0 = [c_region[0:L, (2 + s) * H:(3 + s) * H] for s in range(2)]
        h_flat = h[:, :, :, :].rearrange("p s i t -> p (s i t)")
        tok = h_flat[0:L, 0:GB * SSM].rearrange("p (b d) -> p b d", b=GB)
        tok_sq = h_flat[0:L, GB * SSM:2 * GB * SSM].rearrange("p (b d) -> p b d", b=GB)
        y_t = tmp[0:L, :].rearrange("p (b d) -> p b d", b=GB)
        lin = tmp[:, 0:QI * GT].rearrange("p (i t) -> p i t", i=QI)
        kT = c_region[:, 0:2 * NK * SK].rearrange("p (s k c) -> p s k c", s=2, k=NK)
        rw = c_region[:, 2 * NK * SK:2 * NK * SK + NK * E].rearrange("p (k e) -> p k e", k=NK)
        kv = arena[0:SC, 0:2 * 3 * H].rearrange("p (s c n) -> p s c n", s=2, c=3)
        xs_free = xs[:, 0, :, :].rearrange("p i t -> p (i t)")
        xt = [xs_free[0:L, s * H:(s + 1) * H] for s in range(GB)]
        xn = [xs_free[0:L, (GB + s) * H:(GB + s + 1) * H] for s in range(GB - 1)] + [tmp[0:L, 0:H]]
        q_b = [u_region[:, s * NK * L:(s + 1) * NK * L].rearrange("p (k t) -> p k t", k=NK) for s in range(GB)]
        gate_flat = gate[:, :, :].rearrange("p i t -> p (i t)")
        e_b = [gate_flat[0:L, s * SK:(s + 1) * SK] for s in range(GB)]
        eT = [h_flat[0:SC, s * 3 * L:(s + 1) * 3 * L].rearrange("p (c t) -> p c t", c=3) for s in range(GB)]
        eb = wdt[:, :, :].rearrange("p s d -> p (s d)")
        nrm_flat = nrm[:, :, :, :].rearrange("p g b d -> p (g b d)")
        e_r, rest, w_r = ([nrm_flat[:, (3 * s + k) * E:(3 * s + k + 1) * E] for s in range(GB)] for k in range(3))
        rT = [ssm_t[0:E, s * L:(s + 1) * L] for s in range(GB)]

        Y = [bank(f"y{b}") for b in range(GB)]
        BB = bank("b")
        DB = [bank(f"drive{k}") for k in range(2)]
        ACC = bank("acc")
        TB = Y + [ACC, DB[1]]
        OB = [BB, DB[0]]

        const_in = sem("const_in")
        ident_ok = sem("ident_ok")
        ident_r_ok = sem("ident_r_ok")
        x_in = [sem(f"x_in{s}") for s in range(2)]
        a_exp = sem("a_exp")
        a_ready = sem("a_ready")
        ln_chain = sem("ln_chain")
        mv_ready = sem("mv_ready")
        lv_ready = sem("lv_ready")
        rstd_ready = sem("rstd_ready")
        xn_ready = sem("xn_ready")
        lnT_full = sem("lnT_full")
        lnT_used = sem("lnT_used")
        wf_in = [sem(f"wf_in{s}") for s in range(4)]
        xf_full = sem("xf_full")
        conv_started = sem("conv_started")
        conv_chain = sem("conv_chain")
        raw_copied = sem("raw_copied")
        x_silu = sem("x_silu")
        w_in_sem = [sem(f"w_in{s}") for s in range(2)]
        w_used = sem("w_used")
        wdt_in = [sem(f"wdt_in{s}") for s in range(2)]
        misc_full = sem("misc_full")
        ssm_chain = sem("ssm_chain")
        ssm_rows = sem("ssm_rows")
        sq_ready = sem("sq_ready")
        ms_ready = sem("ms_ready")
        ms_log = sem("ms_log")
        rs_ready = sem("rs_ready")
        nrm_ready = sem("nrm_ready")
        bc_ready = sem("bc_ready")
        c_stored = sem("c_stored")
        c_in = [sem(f"c_in{k}") for k in range(4)]
        abs_done = sem("abs_done")
        lin_done = sem("lin_done")
        soft_exp = sem("soft_exp")
        soft_done = sem("soft_done")
        dt_ready = sem("dt_ready")
        u_ready = sem("u_ready")
        zero_cols = sem("zero_cols")
        decay_ready = sem("decay_ready")
        b_full = sem("b_full")
        drive_done = sem("drive_done")
        scan_done = sem("scan_done")
        hc_done = sem("hc_done")
        yT_done = sem("yT_done")
        y_out = sem("y_out")
        gate_raw = sem("gate_raw")
        gate_silu = sem("gate_silu")
        y_skip = sem("y_skip")
        y_ready = sem("y_ready")
        o_cols = sem("o_cols")
        t_x = [sem(f"t_x{s}") for s in range(GB)]
        t_kT = [sem(f"t_kT{s}") for s in range(2)]
        t_kv = [sem(f"t_kv{s}") for s in range(2)]
        t_out = [sem(f"t_out{s}") for s in range(GB)]
        tail_full = sem("tail_full")
        tail_chain = sem("tail_chain")
        x1_added = sem("x1_added")
        mv1, lv1, rs1, xn1 = (sem(f"tail_{n}1") for n in ("mv", "lv", "rs", "xn"))
        q1_ready = sem("q1_ready")
        max_ready = sem("max_ready")
        e_ready = sem("e_ready")
        eT_ready = sem("eT_ready")
        x2_added = sem("x2_added")
        mv2, lv2, rs2, xn2 = (sem(f"tail_{n}2") for n in ("mv", "lv", "rs", "xn"))
        q2_ready = sem("q2_ready")
        rmax_ready = sem("rmax_ready")
        er_ready = sem("er_ready")
        wr_ready = sem("wr_ready")
        wsum_ready = sem("wsum_ready")
        wT_ready = sem("wT_ready")
        x3_ready = sem("x3_ready")
        mixed = sem("mixed")

        TAIL_READ = {"out": (x1_added, 2), "xT1": (q1_ready, 2), "scores": (e_ready, 1), "eT": (eT_ready, 1),
                     "pv": (x2_added, 2), "xT2": (q2_ready, 2), "logits": (er_ready, 1), "wT": (wT_ready, 1),
                     "mix": (mixed, 2)}

        def misc_read(m):
            what = list(MISC)[m]
            it = NQ * what[1] + what[2] if len(what) > 2 else 0
            return {"ssm": lambda: (ssm_rows, 2 * what[1] + 1), "ssm_tokens": lambda: (ssm_chain, 7 * what[1] + 1),
                    "ssm_back": lambda: (ssm_rows, 2 * what[1] + 2), "dt": lambda: (lin_done, QI * it + what[3] + 1),
                    "y": lambda: (y_skip, QI * it + what[3] + 1)}[what[0]]()

        def acc_read(it, j):
            if j >= 4:
                return gate_raw, QI * it + j - 3
            if it < NQ:
                return raw_copied, QI * it + j + 1
            return o_cols, 2 * (it - NQ) + j // 2 + 1

        def job_source(it, j):
            dq = it % NQ
            if j >= 4:
                return w_in[NI + 4 * dq + j - 4, :, :]
            return w_in[4 * dq + j, :, :] if it < NQ else w_out[4 * dq + j, :, :]

        block = stack.enter_context(nc.Block())

        @block.sync
        def _(sp):
            def load_x(b):
                sp.dma_start(xt0[b % 2], x[b, :, :]).then_inc(x_in[b % 2], 16)

            def load_first(i):
                sp.dma_start(w_first[:, i % 4, :], w_in[i, :, :]).then_inc(wf_in[i % 4], 16)

            def load_weights(n, source):
                if n >= 2:
                    sp.wait_ge(w_used, n - 1)
                sp.dma_start(wr[:, n % 2, 0:source.shape[1]], source).then_inc(w_in_sem[n % 2], 16)

            def load_wdt(it):
                if it >= 2:
                    sp.wait_ge(misc_full, MISC[("dt", (it - 2) // NQ, (it - 2) % NQ, QI - 1)] + 1)
                dq = it % NQ
                sp.dma_start(wdt[:, it % 2, :], w_dt[:, dq * QD:(dq + 1) * QD]).then_inc(wdt_in[it % 2], 16)

            load_x(0)
            load_x(1)
            for t, src in ((cw[:, :, :], conv_w), (cb[:, :], conv_b), (bdt[:, :], b_dt), (dsk[:, :], d_skip),
                           (a_neg[:, :, :], a_log), (rb[:, :], b_router)):
                sp.dma_start(t, src).then_inc(const_in, 16)
            for i in range(4):
                load_first(i)
            for b in range(2, B):
                sp.wait_ge(xn_ready, b - 1)
                load_x(b)
                if b > GB:
                    for i in range(4 * (b - GB), 4 * (b - GB + 1)):
                        sp.wait_ge(xf_full, i - 3)
                        load_first(i)
            for g in range(G):
                for hf in range(2):
                    load_weights(weight_use(NQ * g, 0) - 2 + hf, w_x[hf, :, :])
                load_wdt(NQ * g)
                load_weights(weight_use(NQ * g, 0), job_source(NQ * g, 0))
                sp.wait_ge(ssm_rows, 2 * g + 2)
                sp.dma_start(c_rows[g, :, :], ssm_t[R + NS:SSM, :]).then_inc(c_stored, 16)
                sp.wait_ge(c_stored, 16 * (g + 1))
                if g:
                    sp.wait_ge(hc_done, NQ * STEPS)
                for k in range(4):
                    part = c_rows[g, 4 * k:4 * k + 4, :].rearrange("n t -> (n t)")
                    sp.dma_start(c_region[:, 4 * k * GT:4 * (k + 1) * GT],
                                 part.partition_broadcast(P)).then_inc(c_in[k], 16)
                for dq in range(NQ):
                    it = NQ * g + dq
                    for j in range(8):
                        if j == 4 and dq < NQ - 1:
                            load_wdt(it + 1)
                        if dq or j:
                            load_weights(weight_use(it, j), job_source(it, j))

            def load_kT(b):
                if b >= 2:
                    sp.wait_ge(tail_full, TAIL_AT[("scores", b - 2, 0)] + 1)
                sp.dma_start(kT[:, b % 2, :, :], ctx_t[b, :, :, :]).then_inc(t_kT[b % 2], 16)

            def load_kv(b):
                if b >= 2:
                    sp.wait_ge(tail_full, TAIL_AT[("pv", b - 2, 1)] + 1)
                sp.dma_start(kv[:, b % 2, :, :], ctx[b, :, :].rearrange("(c p) n -> p c n", p=SC))\
                  .then_inc(t_kv[b % 2], 16)

            def load_rows(b):
                sp.dma_start(xt[b % GB], x[b, :, :]).then_inc(t_x[b % GB], 16)

            sp.wait_ge(w_used, weight_use(2 * NQ - 1, 3) + 1)
            for b in range(GB):
                load_rows(b)
            n0 = weight_use(2 * NQ - 1, 7) + 1
            for j in range(2):
                load_weights(n0 + j, w_out[j, :, :])
            sp.wait_ge(hc_done, 2 * NQ * STEPS)
            sp.dma_start(rw, w_router).then_inc(const_in, 16)
            sp.dma_start(eb[0:E, :], e_bias).then_inc(const_in, 16)
            for b in range(2):
                load_kT(b)
                load_kv(b)
            for j in range(2, 2 * NK):
                load_weights(n0 + j, w_out[j, :, :])
                if j in (5, 9, 11):
                    what, b0 = {5: (load_kT, 2), 9: (load_kv, 2), 11: (load_kT, 4)}[j]
                    what(b0)
                    what(b0 + 1)
            load_kv(4)
            load_kv(5)
            for b in range(GB):
                sp.wait_ge(mixed, 2 * b + 2)
                sp.dma_start(out[b, :, :], xt[b]).then_inc(t_out[b], 16)
            for b in range(GB):
                sp.wait_ge(t_out[b], 16)
                load_rows(GB + b)
            for b in (6, 7):
                load_kT(b)
            for b in (6, 7):
                load_kv(b)
            for b in range(GB, B):
                sp.wait_ge(mixed, 2 * b + 2)
                sp.dma_start(out[b, :, :], xt[b % GB]).then_inc(t_out[b % GB], 16)
            for s in range(GB):
                sp.wait_ge(t_out[s], 32)

        @block.gpsimd
        def _(pool):
            pool.memset(ident[:, :], 0.0).then_inc(ident_ok, 1)
            pool.memset(ones[:, :], 1.0)
            pool.memset(eps_ln[:, :], LN_EPS).then_inc(ident_ok, 1)
            pool.wait_ge(ident_ok, 2)
            pool.affine_select(out=ident[:, :], in_=ident[:, :], compare_op=ALU.not_equal, fill=1.0, base=0,
                               pattern=[[-1, P]], channel_multiplier=1).then_inc(ident_ok, 1)
            pool.wait_ge(xf_full, NI)
            pool.memset(decay[:, :, :, :, 0:1].rearrange("p s b i t -> p (s b i) t"), 0.0).then_inc(zero_cols, 1)

            def dt_times_x(it, i):
                g, dq = it // NQ, it % NQ
                pool.wait_ge(dt_ready, QI * it + i + 1)
                if it >= 2:
                    pool.wait_ge(drive_done, (it - 1) * STEPS)
                pool.tensor_tensor(u[:, it % 2, i, :], dt[:, it % 2, i, :], xs[:, g, QI * dq + i, :],
                                   ALU.mult).then_inc(u_ready, 1)

            def y_gate(it, i):
                g, dq = it // NQ, it % NQ
                pool.wait_ge(y_skip, QI * it + i + 1)
                pool.wait_ge(gate_silu, it + 1)
                col = xs[:, g, QI * dq + i, :]
                pool.tensor_tensor(col, col, gate[:, i, :], ALU.mult).then_inc(y_ready, 1)

            for g in range(G):
                for i in range(QI):
                    dt_times_x(NQ * g, i)
                for dq in range(NQ):
                    it = NQ * g + dq
                    for n in range(NS):
                        if dq == 0 and n % 4 == 0:
                            pool.wait_ge(c_in[n // 4], 16 * (g + 1))
                        for b in range(GB):
                            step = it * STEPS + n * GB + b
                            if b == 2 and dq > 0 and 2 <= n < 2 + QI:
                                y_gate(it - 1, n - 2)
                            if b == 2 and dq < NQ - 1 and 11 <= n < 11 + QI:
                                dt_times_x(it + 1, n - 11)
                            pool.wait_ge(scan_done, step + 1)
                            c_n = c_bc[:, n, b * L:(b + 1) * L].unsqueeze(1).to_broadcast([P, QI, L])
                            pool.tensor_tensor(h[:, b, :, :], h[:, b, :, :], c_n, ALU.mult).then_inc(hc_done, 1)
                for i in range(QI):
                    y_gate(NQ * (g + 1) - 1, i)

        @block.scalar
        def _(act):
            def norm_scale(s, count, mv, lv, rs):
                act.wait_ge(mv, count)
                act.activation(stats[:, s, 14:15], stats[:, s, 13:14], ACT.Ln, bias=eps_ln[0:L, :]).then_inc(lv, 1)
                act.wait_ge(lv, count)
                act.activation(stats[:, s, 15:16], stats[:, s, 14:15], ACT.Exp, scale=-0.5).then_inc(rs, 1)

            def conv_start(psum, i, g):
                act.activation(xs[:, g, i, :], psum[:, 0:GT], ACT.Identity,
                               bias=cb[:, i:i + 1], scale=cw[:, i, KC - 1:KC]).then_inc(conv_started, 1)

            def norm_columns(b):
                for half in range(2):
                    act.wait_ge(lnT_full, 2 * b + half + 1)
                    act.copy(xnT[:, 4 * half:4 * half + 4, b * L:(b + 1) * L],
                             Y[2 + half][:, 0:4 * L].rearrange("p (k t) -> p k t", k=4)).then_inc(lnT_used, 1)

            act.preload_act_table_set(LOG_EXP)
            act.wait_ge(ident_ok, 3)
            act.wait_ge(const_in, 16 * 6)
            act.activation(a_neg[:, :, :], a_neg[:, :, :], ACT.Exp).then_inc(a_exp, 1)
            for b in range(GB):
                norm_scale(b % 2, b + 1, mv_ready, lv_ready, rstd_ready)
                norm_columns(b)
            for b in range(GB, B):
                norm_scale(b % 2, b + 1, mv_ready, lv_ready, rstd_ready)
                for i in range(4 * (b - GB), 4 * (b - GB + 1)):
                    act.wait_ge(xf_full, i + 1)
                    conv_start(Y[i % 2], i, 0)
                norm_columns(b)
            act.wait_ge(conv_chain, 3 * NI)
            for dq in range(NQ):
                part = xs[:, 0, QI * dq:QI * (dq + 1), :]
                act.activation(part, part, ACT.Silu).then_inc(x_silu, 1)
            act.preload_act_table_set(LOG_EXP)

            def ssm_norm(g):
                act.wait_ge(misc_full, MISC[("ssm", g)] + 1)
                act.copy(ssm_t[:, :], DB[0][0:SSM, 0:GT]).then_inc(ssm_rows, 1)
                act.wait_ge(ssm_chain, 7 * g + 1)
                act.activation(tok_sq, tok, ACT.Square).then_inc(sq_ready, 1)
                act.wait_ge(ms_ready, g + 1)
                act.activation(ms[:, :, :], ms[:, :, :], ACT.Ln).then_inc(ms_log, 1)
                act.wait_ge(ms_log, g + 1)
                act.activation(ms[:, :, :], ms[:, :, :], ACT.Exp, scale=-0.5).then_inc(rs_ready, 1)
                act.wait_ge(misc_full, MISC[("ssm_back", g)] + 1)
                act.copy(ssm_t[:, :], DB[0][0:SSM, 0:GT]).then_inc(ssm_rows, 1)

            def soft_start(it, i):
                g, dq = it // NQ, it % NQ
                what = ("dt", g, dq, i)
                act.wait_ge(misc_full, MISC[what] + 1)
                act.activation(lin[:, i, :], DB[job_bank(what)][:, 0:GT], ACT.Identity,
                               bias=bdt[:, QI * dq + i:QI * dq + i + 1]).then_inc(lin_done, 1)

            def soft_abs(it):
                act.wait_ge(lin_done, QI * (it + 1))
                if it >= 2:
                    act.wait_ge(u_ready, QI * (it - 1))
                act.activation(dt[:, it % 2, :, :], lin, ACT.Abs).then_inc(abs_done, 1)

            def soft_log(it):
                d = dt[:, it % 2, :, :]
                act.wait_ge(abs_done, it + 1)
                act.activation(d, d, ACT.Exp, scale=-1.0).then_inc(soft_exp, 1)
                act.wait_ge(soft_exp, it + 1)
                act.activation(d, d, ACT.Ln, bias=1.0).then_inc(soft_done, 1)

            def decay_tile(it, n, i):
                state = it * NS + n
                if i == 0:
                    act.wait_ge(dt_ready, QI * (it + 1))
                    if state >= 2:
                        act.wait_ge(scan_done, GB * (state - 1))
                tile = QI * (it % NQ) + i
                a = act.activation(decay[:, state % 2, :, i, 1:L],
                                   dt[:, it % 2, i, :].rearrange("p (b t) -> p b t", b=GB)[:, :, 1:L],
                                   ACT.Exp, scale=a_neg[:, tile, n:n + 1])
                if i == QI - 1:
                    a.then_inc(decay_ready, 1)

            def silus(it):
                act.wait_ge(gate_raw, QI * (it + 1))
                act.activation(gate[:, :, :], gate[:, :, :], ACT.Silu).then_inc(gate_silu, 1)
                if it < NQ:
                    act.wait_ge(conv_chain, 3 * (NI + QI * (it + 1)))
                    part = xs[:, 1, QI * it:QI * (it + 1), :]
                    act.activation(part, part, ACT.Silu).then_inc(x_silu, 1)
                act.preload_act_table_set(LOG_EXP)

            def y_rows(it):
                act.wait_ge(dt_ready, QI * (it + 1))
                for b in range(GB):
                    act.wait_ge(yT_done, (it + 1) * STEPS - GB + b + 1)
                    act.copy(y_t[:, b, :], Y[b][0:L, :]).then_inc(y_out, 1)

            def projected(it, j):
                if it >= NQ and j in (0, 2):
                    return
                act.wait_ge(w_used, weight_use(it, j) + 1)
                if j >= 4:
                    if it:
                        act.wait_ge(y_ready, QI * it)
                    act.copy(gate[:, j - 4, :], ACC[:, 0:GT]).then_inc(gate_raw, 1)
                elif it < NQ:
                    i = QI * it + j
                    act.wait_ge(conv_chain, 3 * (NI + i))
                    act.copy(raw[:, :], ACC[:, 0:GT]).then_inc(raw_copied, 1)
                    act.wait_ge(raw_copied, i + 1)
                    conv_start(raw, i, 1)
                else:
                    act.copy(xnT[:, 2 * (it - NQ) + j // 2, 0:GT], ACC[:, 0:GT]).then_inc(o_cols, 1)

            for g in range(G):
                ssm_norm(g)
                for i in range(QI):
                    soft_start(NQ * g, i)
                soft_abs(NQ * g)
                soft_log(NQ * g)
                if g == 0:
                    act.wait_ge(zero_cols, 1)
                    act.wait_ge(a_ready, 1)
                for i in range(QI):
                    decay_tile(NQ * g, 0, i)
                for dq in range(NQ):
                    it = NQ * g + dq
                    for n in range(NS):
                        for b in range(GB):
                            if n < NS - 1:
                                decay_tile(it, n + 1, b)
                            elif dq < NQ - 1:
                                decay_tile(it + 1, 0, b)
                            if b == 0 and n % 2 == 0 and n:
                                projected(it, n // 2 - 1)
                            if b == 1 and n == 0 and dq:
                                y_rows(it - 1)
                            if b == 2 and dq < NQ - 1:
                                if DT_AT <= n < DT_AT + QI:
                                    soft_start(it + 1, n - DT_AT)
                                if n == DT_AT + QI - 1:
                                    soft_abs(it + 1)
                                if n == DT_AT + QI:
                                    soft_log(it + 1)
                        if n == 0 and dq > 0:
                            silus(it - 1)
                    projected(it, 7)
                y_rows(NQ * (g + 1) - 1)
                silus(NQ * (g + 1) - 1)

            def out_columns(ho):
                act.wait_ge(w_used, weight_use(2 * NQ - 1, 7) + 1 + 2 * (ho + 1))
                act.copy(xnT[:, ho, GT:2 * GT], OB[ho % 2][:, 0:GT]).then_inc(o_cols, 1)

            def columns(what, b, ready):
                for half in range(2):
                    n = TAIL_AT[(what, b, half)]
                    act.wait_ge(tail_full, n + 1)
                    act.copy(q_b[b % GB][:, 4 * half:4 * half + 4, :],
                             TB[n % 6][:, 0:4 * L].rearrange("p (k t) -> p k t", k=4)).then_inc(ready, 1)

            for g in range(G):
                batches = range(GB * g, GB * (g + 1))
                fill = (lambda k: out_columns(k)) if g == 0 else (lambda k: None)
                fill(0)
                for b in batches:
                    norm_scale(b % GB, b + 1, mv1, lv1, rs1)
                for b in batches:
                    columns("xT1", b, q1_ready)
                fill(1)
                for b in batches:
                    n = TAIL_AT[("scores", b, 0)]
                    act.wait_ge(max_ready, b + 1)
                    act.activation(e_b[b % GB], TB[n % 6][0:L, 0:SK], ACT.Exp, bias=sm[:, b % GB, 0:1],
                                   accum_out=sm[:, b % GB, 1:2]).then_inc(e_ready, 1)
                fill(2)
                for b in batches:
                    n = TAIL_AT[("eT", b, 0)]
                    act.wait_ge(tail_full, n + 1)
                    act.copy(eT[b % GB], TB[n % 6][0:SC, 0:3 * L].rearrange("p (c t) -> p c t", c=3))\
                       .then_inc(eT_ready, 1)
                fill(3)
                fill(4)
                for b in batches:
                    norm_scale(b % GB, b + 1, mv2, lv2, rs2)
                for b in batches:
                    columns("xT2", b, q2_ready)
                fill(5)
                for b in batches:
                    n = TAIL_AT[("logits", b, 0)]
                    act.wait_ge(rmax_ready, b + 1)
                    act.activation(e_r[b % GB], TB[n % 6][0:L, 0:E], ACT.Exp, bias=sm[:, b % GB, 3:4],
                                   accum_out=sm[:, b % GB, 4:5]).then_inc(er_ready, 1)
                fill(6)
                for b in batches:
                    n = TAIL_AT[("wT", b, 0)]
                    act.wait_ge(tail_full, n + 1)
                    act.copy(rT[b % GB], TB[n % 6][0:E, 0:L]).then_inc(wT_ready, 1)
                fill(7)

        @block.tensor
        def _(pe):
            def transpose(o, i, last=True, start=True):
                k = i.shape[0]
                return pe.matmul(o, lhsT=i, rhs=ident[0:k, 0:k], start=start, stop=last, is_transpose=True)

            def norm_turn(b):
                pe.wait_ge(xn_ready, b + 1)
                if b:
                    pe.wait_ge(lnT_used, 2 * b)
                for half in range(2):
                    for k in range(4):
                        last = transpose(Y[2 + half][:, k * L:(k + 1) * L],
                                         xn0[b % 2][:, (4 * half + k) * P:(4 * half + k + 1) * P])
                    last.then_inc(lnT_full, 1)

            pe.wait_ge(ident_ok, 3)
            for b in range(GB):
                norm_turn(b)
            pe.wait_ge(lnT_used, 2 * GB)
            for b in range(GB, B):
                for i in range(4 * (b - GB), 4 * (b - GB + 1)):
                    pe.wait_ge(wf_in[i % 4], 16 * (i // 4 + 1))
                    if i >= 2:
                        pe.wait_ge(conv_chain, 3 * (i - 1))
                    for k in range(NK):
                        last = pe.matmul(Y[i % 2][:, 0:GT], lhsT=w_first[:, i % 4, k * P:(k + 1) * P],
                                         rhs=xnT[:, k, 0:GT], start=(k == 0), stop=(k == NK - 1))
                    last.then_inc(xf_full, 1)
                norm_turn(b)
            pe.wait_ge(lnT_used, 2 * B)

            def small(what, beside=None):
                m = MISC[what]
                if beside is not None:
                    pe.wait_ge(scan_done, beside + 1)
                elif what[0] == "y" and what[-1] < 2:
                    pe.wait_ge(scan_done, NQ * (what[1] + 1) * STEPS)
                elif m >= 2:
                    pe.wait_ge(*misc_read(m - 2))
                return DB[job_bank(what)]

            def ssm_steps(g):
                bank_ = small(("ssm", g))
                first = weight_use(NQ * g, 0) - 2
                for i in range(NI):
                    n = first + i // 8
                    if i % 8 == 0:
                        pe.wait_ge(w_in_sem[n % 2], 16 * (n // 2 + 1))
                    if i % QI == 0:
                        pe.wait_ge(x_silu, NQ * g + i // QI + 1)
                    last = pe.matmul(bank_[0:SSM, 0:GT], lhsT=wr[:, n % 2, (i % 8) * SSM:(i % 8 + 1) * SSM],
                                     rhs=xs[:, g, i, :], start=(i == 0), stop=(i == NI - 1))
                    if i == 7:
                        last.then_inc(w_used, 1)
                last.then_inc(misc_full, 1)
                pe.wait_ge(misc_full, MISC[("ssm", g)] + 1)
                pe.sem_inc(w_used, 1)
                bank_ = small(("ssm_tokens", g))
                pe.wait_ge(ssm_rows, 2 * g + 1)
                for b in range(GB):
                    last = transpose(bank_[0:L, b * SSM:(b + 1) * SSM], ssm_t[:, b * L:(b + 1) * L])
                last.then_inc(misc_full, 1)
                bank_ = small(("ssm_back", g))
                pe.wait_ge(nrm_ready, g + 1)
                for b in range(GB):
                    last = transpose(bank_[0:SSM, b * L:(b + 1) * L], nrm[:, g, b, :])
                last.then_inc(misc_full, 1)

            def dt_tile(it, i, beside=None):
                bank_ = small(("dt", it // NQ, it % NQ, i), beside)
                pe.wait_ge(wdt_in[it % 2], 16 * (it // 2 + 1))
                pe.matmul(bank_[:, 0:GT], lhsT=wdt[:, it % 2, i * P:(i + 1) * P], rhs=ssm_t[0:R, :],
                          start=True, stop=True).then_inc(misc_full, 1)

            def y_tile(it, i, beside=None):
                bank_ = small(("y", it // NQ, it % NQ, i), beside)
                pe.wait_ge(y_out, GB * (it + 1))
                for b in range(GB):
                    last = transpose(bank_[:, b * L:(b + 1) * L], y_t[:, b, i * P:(i + 1) * P])
                last.then_inc(misc_full, 1)

            def b_all(it, n):
                step = it * STEPS + n * GB
                if step:
                    pe.wait_ge(drive_done, step)
                one_row = ident_r[:, R + n:R + n + 1].to_broadcast([SSM, P])
                pe.matmul(BB[:, 0:GT], lhsT=one_row, rhs=bc_hi[:, :], start=True, stop=False)
                pe.matmul(BB[:, 0:GT], lhsT=one_row, rhs=bc_lo[:, :], start=False, stop=True).then_inc(b_full, 1)

            def sum_states(step):
                it, n, b = step // STEPS, step % STEPS // GB, step % GB
                pe.wait_ge(hc_done, step + 1)
                if n == 0 and it:
                    pe.wait_ge(y_out, GB * (it - 1) + b + 1)
                for i in range(QI):
                    last = transpose(Y[b][0:L, i * P:(i + 1) * P], h[:, b, i, :],
                                     last=(n == NS - 1 and i == QI - 1), start=(n == 0 and i == 0))
                last.then_inc(yT_done, 1)

            def projection(it, j, k):
                g = it // NQ
                n = weight_use(it, j)
                opens = not (g and j in (1, 3))
                if k == 0:
                    pe.wait_ge(w_in_sem[n % 2], 16 * (n // 2 + 1))
                    if opens and acc_before(it, j):
                        pe.wait_ge(*acc_read(*acc_before(it, j)))
                if j >= 4 or g == 0:
                    rhs = xnT[:, k, GT:2 * GT] if g or j < 4 else xnT[:, k, 0:GT]
                else:
                    rhs = xs[:, 0, 8 * (j % 2) + k, :]
                closes = k == NK - 1 and not (g and j in (0, 2))
                last = pe.matmul(ACC[:, 0:GT], lhsT=wr[:, n % 2, k * P:(k + 1) * P], rhs=rhs,
                                 start=(k == 0 and opens), stop=closes)
                if k == NK - 1:
                    last.then_inc(w_used, 1)

            for g in range(G):
                ssm_steps(g)
                pe.wait_ge(ssm_rows, 2 * g + 2)
                for i in range(QI):
                    dt_tile(NQ * g, i)
                pe.wait_ge(bc_ready, 2 * (g + 1))
                b_all(NQ * g, 0)
                if g == 1:
                    pe.wait_ge(y_ready, NQ * QI)
                for dq in range(NQ):
                    it = NQ * g + dq
                    for n in range(NS):
                        for b in range(GB):
                            step = it * STEPS + n * GB + b
                            if b == 3 and (n < NS - 1 or dq < NQ - 1):
                                b_all(it + (n + 1) // NS, (n + 1) % NS)
                            if b == 2 and dq > 0 and Y_AT <= n < Y_AT + QI:
                                y_tile(it - 1, n - Y_AT, step - 1)
                            if b == 2 and dq < NQ - 1 and DT_AT <= n < DT_AT + QI:
                                dt_tile(it + 1, n - DT_AT, step - 1)
                            if step - LAG >= NQ * g * STEPS:
                                sum_states(step - LAG)
                            j, q = n // 2, n % 2 * GB + b
                            if q:
                                projection(it, j, q - 1)
                            if q == 7:
                                projection(it, j, 7)
                for step in range(NQ * (g + 1) * STEPS - LAG, NQ * (g + 1) * STEPS):
                    sum_states(step)
                for i in range(QI):
                    y_tile(NQ * (g + 1) - 1, i)

            def output_tile(ho):
                if ho >= 2:
                    pe.wait_ge(o_cols, NK + ho - 1)
                for hf in range(2):
                    n = weight_use(2 * NQ - 1, 7) + 1 + 2 * ho + hf
                    pe.wait_ge(w_in_sem[n % 2], 16 * (n // 2 + 1))
                    for k in range(8):
                        last = pe.matmul(OB[ho % 2][:, 0:GT], lhsT=wr[:, n % 2, k * P:(k + 1) * P],
                                         rhs=xs[:, 1, 8 * hf + k, :], start=(hf == 0 and k == 0),
                                         stop=(hf == 1 and k == 7))
                    last.then_inc(w_used, 1)

            def tail_bank(what, b, part=0):
                n = TAIL_AT[(what, b, part)]
                if n >= 6:
                    w, bb, k = TAIL[n - 6]
                    read, parts = TAIL_READ[w]
                    pe.wait_ge(read, parts * bb + k + 1)
                return TB[n % 6]

            def turn_rows(what, b, ready):
                pe.wait_ge(ready, b + 1)
                for half in range(2):
                    bank_ = tail_bank(what, b, half)
                    for k in range(4):
                        last = transpose(bank_[:, k * L:(k + 1) * L],
                                         xn[b % GB][:, (4 * half + k) * P:(4 * half + k + 1) * P])
                    last.then_inc(tail_full, 1)

            pe.wait_ge(y_ready, 2 * NQ * QI)
            for g in range(G):
                batches = range(GB * g, GB * (g + 1))
                fill = (lambda k: output_tile(k)) if g == 0 else (lambda k: None)
                pe.wait_ge(o_cols, NK * (g + 1))
                for b in batches:
                    for half in range(2):
                        bank_ = tail_bank("out", b, half)
                        for k in range(4):
                            last = transpose(bank_[0:L, k * P:(k + 1) * P], xnT[:, 4 * half + k, b * L:(b + 1) * L])
                        last.then_inc(tail_full, 1)
                fill(0)
                for b in batches:
                    turn_rows("xT1", b, xn1)
                fill(1)
                for b in batches:
                    bank_ = tail_bank("scores", b)
                    pe.wait_ge(q1_ready, 2 * b + 2)
                    pe.wait_ge(t_kT[b % 2], 16 * (b // 2 + 1))
                    for k in range(NK):
                        last = pe.matmul(bank_[0:L, 0:SK], lhsT=q_b[b % GB][:, k, :], rhs=kT[:, b % 2, k, :],
                                         start=(k == 0), stop=(k == NK - 1))
                    last.then_inc(tail_full, 1)
                fill(2)
                for b in batches:
                    bank_ = tail_bank("eT", b)
                    pe.wait_ge(e_ready, b + 1)
                    for k in range(3):
                        last = transpose(bank_[0:SC, k * L:(k + 1) * L], e_b[b % GB][:, k * SC:(k + 1) * SC])
                    last.then_inc(tail_full, 1)
                fill(3)
                for b in batches:
                    pe.wait_ge(eT_ready, b + 1)
                    pe.wait_ge(t_kv[b % 2], 16 * (b // 2 + 1))
                    for half in range(2):
                        bank_ = tail_bank("pv", b, half)
                        for k in range(3):
                            last = pe.matmul(bank_[0:L, :], lhsT=eT[b % GB][:, k, :],
                                             rhs=kv[:, b % 2, k, half * 512:(half + 1) * 512],
                                             start=(k == 0), stop=(k == 2))
                        last.then_inc(tail_full, 1)
                fill(4)
                for b in batches:
                    turn_rows("xT2", b, xn2)
                fill(5)
                if g == 0:
                    pe.wait_ge(const_in, 16 * 8)
                for b in batches:
                    bank_ = tail_bank("logits", b)
                    pe.wait_ge(q2_ready, 2 * b + 2)
                    for k in range(NK):
                        pe.matmul(bank_[0:L, 0:E], lhsT=q_b[b % GB][:, k, :], rhs=rw[:, k, :],
                                  start=(k == 0), stop=False)
                    pe.matmul(bank_[0:L, 0:E], lhsT=ones[:, :], rhs=rb[:, :], start=False, stop=True)\
                      .then_inc(tail_full, 1)
                fill(6)
                for b in batches:
                    bank_ = tail_bank("wT", b)
                    pe.wait_ge(wr_ready, b + 1)
                    transpose(bank_[0:E, 0:L], w_r[b % GB]).then_inc(tail_full, 1)
                fill(7)
                for b in batches:
                    pe.wait_ge(wT_ready, b + 1)
                    for half in range(2):
                        bank_ = tail_bank("mix", b, half)
                        pe.matmul(bank_[0:L, :], lhsT=rT[b % GB], rhs=eb[0:E, half * 512:(half + 1) * 512],
                                  start=True, stop=True).then_inc(tail_full, 1)

        @block.vector
        def _(dve):
            def link(ins, chain, count):
                count[0] += 1
                ins.then_inc(chain, 1)
                dve.wait_ge(chain, count[0])

            ln_count = [0]
            conv_count = [0]
            tail_count = [0]

            def norm_stats(rows, s, ready, chain, count):
                link(dve.bn_stats(stats[:, s, 0:6], rows[:, 0:512]), chain, count)
                link(dve.bn_stats(stats[:, s, 6:12], rows[:, 512:1024]), chain, count)
                dve.bn_aggr(stats[:, s, 12:14], stats[:, s, 0:12]).then_inc(ready, 1)

            def norm_apply(normed, rows, s, count, rs, ready):
                dve.wait_ge(rs, count)
                dve.tensor_scalar(normed, rows, stats[:, s, 12:13], stats[:, s, 15:16],
                                  ALU.subtract, ALU.mult).then_inc(ready, 1)

            def norm_row(b):
                s = b % 2
                dve.wait_ge(x_in[s], 16 * (b // 2 + 1))
                norm_stats(xt0[s], s, mv_ready, ln_chain, ln_count)
                if b >= 2:
                    dve.wait_ge(lnT_full, 2 * (b - 1))
                norm_apply(xn0[s], xt0[s], s, b + 1, rstd_ready, xn_ready)

            def conv(psum, i, g):
                dve.wait_ge(conv_started, NI * g + i + 1)
                col = xs[:, g, i, :].rearrange("p (b t) -> p b t", b=GB)
                raw = psum[:, 0:GT].rearrange("p (b t) -> p b t", b=GB)
                for back in range(1, KC):
                    ins = dve.scalar_tensor_tensor(col[:, :, back:L], raw[:, :, 0:L - back],
                                                   cw[:, i, KC - 1 - back:KC - back], col[:, :, back:L],
                                                   ALU.mult, ALU.add)
                    link(ins, conv_chain, conv_count)

            dve.wait_ge(ident_ok, 3)
            dve.tensor_copy(ident_r[:, :], ident[0:SSM, 0:SSM]).then_inc(ident_r_ok, 1)
            for b in range(GB):
                norm_row(b)
            dve.wait_ge(a_exp, 1)
            dve.tensor_scalar(a_neg[:, :, :], a_neg[:, :, :], -1.0, None, ALU.mult).then_inc(a_ready, 1)
            for b in range(GB, B):
                norm_row(b)
                for i in range(4 * (b - GB), 4 * (b - GB + 1)):
                    conv(Y[i % 2], i, 0)

            def ssm_norm(g):
                count = [7 * g]
                dve.wait_ge(misc_full, MISC[("ssm_tokens", g)] + 1)
                link(dve.tensor_copy(tok, DB[1][0:L, 0:GB * SSM].rearrange("p (b d) -> p b d", b=GB)), ssm_chain, count)
                dve.wait_ge(sq_ready, g + 1)
                parts = ((0, R), (R, R + NS), (R + NS, SSM))
                for k, (a, z) in enumerate(parts):
                    link(dve.reduce_sum(ms[:, k, :], tok_sq[:, :, a:z], AX.X), ssm_chain, count)
                link(dve.tensor_scalar(ms[:, 0, :], ms[:, 0, :], 1.0 / R, RMS_EPS, ALU.mult, ALU.add), ssm_chain, count)
                dve.tensor_scalar(ms[:, 1:3, :], ms[:, 1:3, :], 1.0 / NS, RMS_EPS, ALU.mult, ALU.add)\
                   .then_inc(ms_ready, 1)
                dve.wait_ge(rs_ready, g + 1)
                for k, (a, z) in enumerate(parts):
                    ins = dve.tensor_tensor(nrm[:, g, :, a:z], tok[:, :, a:z],
                                            ms[:, k, :].unsqueeze(2).to_broadcast([L, GB, z - a]), ALU.mult)
                    if k < 2:
                        link(ins, ssm_chain, count)
                ins.then_inc(nrm_ready, 1)
                dve.wait_ge(ssm_rows, 2 * g + 2)
                dve.tensor_copy(bc_hi[:, :], ssm_t[:, :]).then_inc(bc_ready, 1)
                dve.wait_ge(bc_ready, 2 * g + 1)
                dve.tensor_tensor(bc_lo[:, :], ssm_t[:, :], bc_hi[:, :].bitcast(F32), ALU.subtract)\
                   .then_inc(bc_ready, 1)

            def soft_add(it, i):
                dve.wait_ge(soft_done, it + 1)
                d = dt[:, it % 2, i, :]
                dve.scalar_tensor_tensor(d, lin[:, i, :], 0.0, d, ALU.max, ALU.add).then_inc(dt_ready, 1)

            def y_tile(it, i):
                g, dq = it // NQ, it % NQ
                tile = QI * dq + i
                col = xs[:, g, tile, :]
                dve.wait_ge(misc_full, MISC[("y", g, dq, i)] + 1)
                dve.scalar_tensor_tensor(col, col, dsk[:, tile:tile + 1], DB[job_bank(("y", g, dq, i))][:, 0:GT], ALU.mult, ALU.add)\
                   .then_inc(y_skip, 1)

            def drive(it, n, b):
                step = it * STEPS + n * GB + b
                if b == 0:
                    dve.wait_ge(b_full, it * NS + n + 1)
                if last_in_bank(step) is not None:
                    dve.wait_ge(scan_done, last_in_bank(step) + 1)
                if b == 1 and n and narrow(it, n - 1):
                    i = n - 1 - DT_AT
                    if i >= 0:
                        dve.wait_ge(lin_done, QI * (it + 1) + i + 1)
                    else:
                        dve.wait_ge(y_skip, QI * (it - 1) + n - Y_AT)
                b_n = BB[:, b * L:(b + 1) * L].unsqueeze(1).to_broadcast([P, QI, L])
                dve.tensor_tensor(DB[drive_bank(it, n, b)][:, 0:QI * L].rearrange("p (i t) -> p i t", i=QI),
                                  u[:, it % 2, :, b * L:(b + 1) * L], b_n, ALU.mult).then_inc(drive_done, 1)

            def scan(it, n, b):
                step = it * STEPS + n * GB + b
                if b == 0:
                    dve.wait_ge(decay_ready, it * NS + n + 1)
                if step >= 4:
                    dve.wait_ge(yT_done, step - 3)
                dve.wait_ge(drive_done, step + 1)
                dve.tensor_tensor_scan(h[:, b, :, :].rearrange("p i t -> p (i t)"),
                                       decay[:, (it * NS + n) % 2, b, :, :].rearrange("p i t -> p (i t)"),
                                       DB[drive_bank(it, n, b)][:, 0:QI * L], 0.0, ALU.mult, ALU.add)\
                   .then_inc(scan_done, 1)

            def tap(i, back, g=1):
                if back == 1:
                    dve.wait_ge(conv_started, NI * g + i + 1)
                else:
                    dve.wait_ge(conv_chain, 3 * (NI * g + i) + back - 1)
                col = xs[:, g, i, :].rearrange("p (b t) -> p b t", b=GB)
                before = raw[:, :].rearrange("p (b t) -> p b t", b=GB)
                dve.scalar_tensor_tensor(col[:, :, back:L], before[:, :, 0:L - back],
                                         cw[:, i, KC - 1 - back:KC - back], col[:, :, back:L],
                                         ALU.mult, ALU.add).then_inc(conv_chain, 1)

            dve.wait_ge(zero_cols, 1)
            for g in range(G):
                ssm_norm(g)
                for i in range(QI):
                    soft_add(NQ * g, i)
                for dq in range(NQ):
                    it = NQ * g + dq
                    dve.wait_ge(u_ready, QI * (it + 1))
                    for n in range(NS):
                        drive(it, n, 0)
                        drive(it, n, 1)
                        scan(it, n, 0)
                        scan(it, n, 1)
                        if g == 0 and 2 <= n < 10:
                            tap(QI * it + n // 2 - 1, 3 if n % 2 else 1)
                        if dq < NQ - 1 and 10 <= n < 10 + QI:
                            soft_add(it + 1, n - 10)
                        if narrow(it, n):
                            drive(it, n, 2)
                            scan(it, n, 2)
                            drive(it, n, 3)
                            if dq > 0 and n < Y_AT + QI:
                                y_tile(it - 1, n - Y_AT)
                            scan(it, n, 3)
                        else:
                            drive(it, n, 2)
                            drive(it, n, 3)
                            scan(it, n, 2)
                            scan(it, n, 3)
                        if g == 0 and 2 <= n < 10 and n % 2 == 0:
                            tap(QI * it + n // 2 - 1, 2)
                for i in range(QI):
                    y_tile(NQ * (g + 1) - 1, i)

            for g in range(G):
                batches = range(GB * g, GB * (g + 1))
                for b in batches:
                    s = b % GB
                    dve.wait_ge(t_x[s], 16 * (g + 1))
                    for half in range(2):
                        n = TAIL_AT[("out", b, half)]
                        part = xt[s][:, half * 512:(half + 1) * 512]
                        dve.wait_ge(tail_full, n + 1)
                        dve.tensor_tensor(part, part, TB[n % 6][0:L, :], ALU.add).then_inc(x1_added, 1)
                    dve.wait_ge(x1_added, 2 * b + 2)
                    norm_stats(xt[s], s, mv1, tail_chain, tail_count)
                for b in batches:
                    norm_apply(xn[b % GB], xt[b % GB], b % GB, b + 1, rs1, xn1)
                for b in batches:
                    n = TAIL_AT[("scores", b, 0)]
                    dve.wait_ge(tail_full, n + 1)
                    dve.reduce_max(sm[:, b % GB, 0:1], TB[n % 6][0:L, 0:SK], AX.X, negate=True).then_inc(max_ready, 1)
                for b in batches:
                    dve.wait_ge(e_ready, b + 1)
                    link(dve.reciprocal(sm[:, b % GB, 2:3], sm[:, b % GB, 1:2]), tail_chain, tail_count)
                for b in batches:
                    s = b % GB
                    for half in range(2):
                        n = TAIL_AT[("pv", b, half)]
                        part = xt[s][:, half * 512:(half + 1) * 512]
                        dve.wait_ge(tail_full, n + 1)
                        dve.scalar_tensor_tensor(part, TB[n % 6][0:L, :], sm[:, s, 2:3], part,
                                                 ALU.mult, ALU.add).then_inc(x2_added, 1)
                    dve.wait_ge(x2_added, 2 * b + 2)
                    norm_stats(xt[s], s, mv2, tail_chain, tail_count)
                for b in batches:
                    norm_apply(xn[b % GB], xt[b % GB], b % GB, b + 1, rs2, xn2)
                for b in batches:
                    n = TAIL_AT[("logits", b, 0)]
                    dve.wait_ge(tail_full, n + 1)
                    dve.reduce_max(sm[:, b % GB, 3:4], TB[n % 6][0:L, 0:E], AX.X, negate=True).then_inc(rmax_ready, 1)
                for b in batches:
                    s = b % GB
                    dve.wait_ge(er_ready, b + 1)
                    link(dve.max(sm[:, s, 8:16], e_r[s]), tail_chain, tail_count)
                    link(dve.match_replace(rest[s], sm[:, s, 8:16], e_r[s], -1.0), tail_chain, tail_count)
                    link(dve.scalar_tensor_tensor(w_r[s], rest[s], 0.0, e_r[s], ALU.max, ALU.subtract),
                         tail_chain, tail_count)
                    link(dve.reciprocal(sm[:, s, 5:6], sm[:, s, 4:5]), tail_chain, tail_count)
                    dve.tensor_scalar(w_r[s], w_r[s], sm[:, s, 5:6], -1.0, ALU.mult, ALU.mult).then_inc(wr_ready, 1)
                for b in batches:
                    s = b % GB
                    dve.wait_ge(wr_ready, b + 1)
                    dve.reduce_sum(sm[:, s, 6:7], w_r[s], AX.X).then_inc(wsum_ready, 1)
                    dve.wait_ge(wsum_ready, b + 1)
                    dve.scalar_tensor_tensor(xt[s], xn[s], sm[:, s, 6:7], xt[s], ALU.mult, ALU.add)\
                       .then_inc(x3_ready, 1)
                for b in batches:
                    s = b % GB
                    dve.wait_ge(x3_ready, b + 1)
                    for half in range(2):
                        n = TAIL_AT[("mix", b, half)]
                        part = xt[s][:, half * 512:(half + 1) * 512]
                        dve.wait_ge(tail_full, n + 1)
                        dve.tensor_tensor(part, part, TB[n % 6][0:L, :], ALU.add).then_inc(mixed, 1)


def kernel(**inputs):
    import numpy as np
    import concourse.bacc as bacc
    from concourse.bass_utils import run_bass_kernel_spmd

    a = {k: np.asarray(v) for k, v in inputs.items()}

    def tiles(w, rows):
        o, i = w.shape
        return w.reshape(o // rows, rows, i // 1024, 8, P).transpose(0, 2, 4, 3, 1).reshape(-1, P, 8 * rows)

    def channels(v):
        return v.reshape(NI, P, -1).transpose(1, 0, 2)

    arrays = {
        "x": a["x"],
        "ctx": a["ctx_4096"],
        "ctx_t": a["ctx_4096"].reshape(B, SK, NK, P).transpose(0, 3, 2, 1),
        "w_in": tiles(a["L0_attn_W_in"], P),
        "w_out": tiles(a["L0_attn_W_out"], P),
        "w_x": tiles(a["L0_attn_W_x"], SSM),
        "w_dt": a["L0_attn_W_dt"].T,
        "conv_w": channels(a["L0_attn_conv_w"]),
        "conv_b": channels(a["L0_attn_conv_b"])[:, :, 0],
        "b_dt": channels(a["L0_attn_b_dt"])[:, :, 0],
        "a_log": channels(a["L0_attn_A_log"]),
        "d_skip": channels(a["L0_attn_D"])[:, :, 0],
        "w_router": a["L0_ffn_router_weight"].reshape(E, NK, P).transpose(2, 1, 0),
        "b_router": a["L0_ffn_router_bias"].reshape(1, E),
        "e_bias": a["L0_ffn_expert_bias"],
    }
    arrays = {k: np.ascontiguousarray(v) for k, v in arrays.items()}
    nc = bacc.Bacc("TRN2", target_bir_lowering=False, num_devices=1)
    args = [nc.dram_tensor(k, v.shape, F32, kind="ExternalInput").ap() for k, v in arrays.items()]
    args.append(nc.dram_tensor("out", (B, L, H), F32, kind="ExternalOutput").ap())
    decoder_layer(nc, *args)
    r = run_bass_kernel_spmd(nc, [arrays], core_ids=[0])
    return r.results[0]["out"]
```

```python
import concourse.bass as bass
from concourse import mybir
from contextlib import ExitStack

F32 = mybir.dt.float32
ALU = mybir.AluOpType
ACT = mybir.ActivationFunctionType
AX = mybir.AxisListType

B, L, H = 8, 112, 1024
DI, NS, R, KC = 2048, 16, 64, 4
SK = 375
E = 64
P = 128
G, GB = 2, 4
GT = GB * L
NI, NK = DI // P, H // P
NQ, QI = 4, 4
QD = QI * P
SSM = R + 2 * NS
SC = SK // 3
LN_EPS, RMS_EPS = 1e-5, 1e-6
LAG = 3
STEPS = NS * GB
EARLY = 4
LATE = 2
HS = 6
AFTER = 2
U_PAIRS = {3: 30}
LOG_EXP = "natural_log_exp_and_others"


def quad_plan(it):
    g, dq = it // NQ, it % NQ
    y = [("y", (it - 1) // NQ, (it - 1) % NQ, i) for i in range(QI)] if it else []
    dt = [("dt", (it + 1) // NQ, (it + 1) % NQ, i) for i in range(QI)] if it < G * NQ - 1 else []
    gates = [("gate", g, QI * dq + i) for i in range(QI)]
    if it == NQ - 1:
        return [(y[i], 3 + i, 3 + i) for i in range(QI)] + [
            (("ssm", 1), 12, 23), (("ssm_tokens", 1), 25, 25), (gates[0], 28, 33), (("ssm_back", 1), 36, 36)] + [
            (dt[i], 38 + i, 38 + i) for i in range(QI)] + [
            (gates[1], 42, 48), (gates[2], 50, 56), (gates[3], 58, 63)]
    if it == NQ:
        return [(y[i], 3 + i, 3 + i) for i in range(QI)] + [
            (gates[0], 8, 14), (gates[1], 16, 22), (dt[0], 23, 23), (dt[1], 24, 24), (gates[2], 26, 32),
            (dt[2], 33, 33), (dt[3], 34, 34), (gates[3], 36, 42), (("out", 1, 0), 44, 50), (("out", 1, 1), 52, 58)]
    first = EARLY + QI * it if g == 0 else 2 + QI * (it - NQ - 1)
    jobs = [("out" if g else "x", g, first + i) for i in range(QI)] + gates
    small = {1: y[:2], 2: y[2:], 3: dt[:2], 4: dt[2:]}
    plan = []
    for p, job in enumerate(jobs):
        two = small.get(p, [])
        plan += [(what, 8 * p + i, 8 * p + i) for i, what in enumerate(two)]
        plan += [(job, 8 * p + (3 if two else 1), 8 * p + 7)]
    return plan


PLAN = [quad_plan(it) for it in range(G * NQ)]
ACC_ORDER = ([("x", 0, i) for i in range(EARLY)] + [what for plan in PLAN for what, _, _ in plan] +
             [("out", 1, NI - LATE + i) for i in range(LATE)])
RING = []
for _what in [("ssm", 0)] + ACC_ORDER:
    if _what[0] == "ssm":
        RING += [("W_x", _what[1], 0), ("W_x", _what[1], 1)]
    elif _what[0] in ("x", "gate", "out"):
        RING += [_what]
WEIGHT_USE = {_what: _n for _n, _what in enumerate(RING)}
MISC = {_what: _n for _n, _what in enumerate(
    [("ssm", 0), ("ssm_tokens", 0), ("ssm_back", 0)] + [("dt", 0, 0, i) for i in range(QI)] +
    [what for what in ACC_ORDER if what[0] not in ("x", "gate", "out")] +
    [("y", G - 1, NQ - 1, i) for i in range(QI)])}


def matmul_steps(first, last, count):
    return [last - (count - 1 - k) * (last - first + 1) // count for k in range(count)]


FROM_PE = {}
for _it, _plan in enumerate(PLAN):
    for _what, _, _last in _plan:
        FROM_PE.setdefault(_it * STEPS + _last + AFTER, []).append(_what)


def job_bank(what):
    kind, i = what[0], what[-1]
    return (i + 1) % 2 if kind in ("y", "dt") else {"ssm": 0, "ssm_tokens": 1, "ssm_back": 0}[kind]


def y_pairs(it):
    return (2, 3, 4, 5) if it in (NQ - 1, NQ) else (7, 8, 11, 12)


def y_steps(it):
    return (14, 16, 18, 20) if it in (NQ - 1, NQ) else (20, 22, 27, 30)


def soft_pairs(it):
    return (26, 27, 28, 29) if it == NQ - 1 else (25, 26, 28, 29)


def u_steps(it):
    return (54, 57, 60, 62) if it == NQ - 1 else (52, 56, 59, 62)


def silu_at(it):
    return 2 if it in (NQ - 1, NQ) else 3


def soft_at(it):
    return 10 if it == NQ - 1 else 9


def tail_uses():
    order = []
    for g in range(G):
        for what, parts in (("out", 2), ("xT1", 2), ("scores", 1), ("eT", 1), ("pv", 2), ("xT2", 2), ("logits", 1),
                            ("wT", 1), ("mix", 2)):
            order += [(what, b, k) for b in range(GB * g, GB * (g + 1)) for k in range(parts)]
    return order


TAIL = tail_uses()
TAIL_AT = {what: n for n, what in enumerate(TAIL)}


def decoder_layer(nc, x, ctx, ctx_t, w_in, w_out, w_x, w_dt, conv_w, conv_b, b_dt, a_log, d_skip,
                  w_router, b_router, e_bias, out):
    bc_rows = nc.dram_tensor("bc_rows", (G, 2 * NS, GT), F32, kind="Internal").ap()
    with ExitStack() as stack:
        def sb(name, shape, dtype=F32):
            return stack.enter_context(nc.sbuf_tensor(name, shape, dtype))

        def bank(name):
            return stack.enter_context(nc.psum_tensor(name, [P, 512], F32))

        def sem(name):
            return stack.enter_context(nc.semaphore(name))

        xs = sb("xs", [P, G, NI, GT])
        xnT = sb("xnT", [P, NK, B * L])
        c_region = sb("c_region", [P, NS * GT])
        arena = sb("arena", [P, 4 * QI * GT])
        u_region = sb("u_region", [P, 2 * QI * GT])
        gate = sb("gate", [P, QI, GT])
        tmp = sb("tmp", [P, GB * QD])
        h = sb("h", [P, HS, QI, L])
        raw = sb("raw", [P, GT])
        y_side = sb("y_side", [P, 2, GT])
        wr = sb("wr", [P, 2, NK * P])
        wdt = sb("wdt", [R, 2, QD])
        ident = sb("ident", [P, P])
        ssm_t = sb("ssm_t", [SSM, GT])
        b_ring = sb("b_ring", [P, 2, GT])
        nrm = sb("nrm", [L, GB, SSM])
        ms = sb("ms", [L, 3, GB])
        stats = sb("stats", [L, GB, 16])
        sm = sb("sm", [L, GB, 16])
        cw = sb("cw", [P, NI, KC])
        cb = sb("cb", [P, NI])
        bdt = sb("bdt", [P, NI])
        dsk = sb("dsk", [P, NI])
        a_neg = sb("a_neg", [P, NI, NS])
        rb = sb("rb", [1, E])
        ones = sb("ones", [1, L])
        eps_ln = sb("eps_ln", [P, 1])

        c_bc = c_region[:, :].rearrange("p (n t) -> p n t", n=NS)
        w_first = arena[:, 0:4 * NK * P].rearrange("p (s n) -> p s n", s=4)
        dt = arena[:, 0:2 * QI * GT].rearrange("p (s i t) -> p s i t", s=2, i=QI)
        decay = arena[:, 2 * QI * GT:].rearrange("p (s b i t) -> p s b i t", s=2, b=GB, i=QI)
        u = u_region[:, :].rearrange("p (s i t) -> p s i t", s=2, i=QI)
        xt0 = [c_region[0:L, s * H:(s + 1) * H] for s in range(4)]
        xn0 = [c_region[0:L, (4 + s) * H:(5 + s) * H] for s in range(3)]
        h_flat = h[:, :, :, :].rearrange("p s i t -> p (s i t)")
        tok = tmp[0:L, 0:GB * SSM].rearrange("p (b d) -> p b d", b=GB)
        tok_sq = tmp[0:L, GB * SSM:2 * GB * SSM].rearrange("p (b d) -> p b d", b=GB)
        y_t = tmp[0:L, :].rearrange("p (b d) -> p b d", b=GB)
        lin = tmp[:, 0:QI * GT].rearrange("p (i t) -> p i t", i=QI)
        kT = c_region[:, 0:2 * NK * SK].rearrange("p (s k c) -> p s k c", s=2, k=NK)
        rw = c_region[:, 2 * NK * SK:2 * NK * SK + NK * E].rearrange("p (k e) -> p k e", k=NK)
        kv = arena[0:SC, 0:2 * 3 * H].rearrange("p (s c n) -> p s c n", s=2, c=3)
        xs_free = xs[:, 0, :, :].rearrange("p i t -> p (i t)")
        xt = [xs_free[0:L, s * H:(s + 1) * H] for s in range(GB)]
        xn = [xs_free[0:L, (GB + s) * H:(GB + s + 1) * H] for s in range(GB - 1)] + [tmp[0:L, 0:H]]
        q_b = [u_region[:, s * NK * L:(s + 1) * NK * L].rearrange("p (k t) -> p k t", k=NK) for s in range(GB)]
        gate_flat = gate[:, :, :].rearrange("p i t -> p (i t)")
        e_b = [gate_flat[0:L, s * SK:(s + 1) * SK] for s in range(GB)]
        eT = [h_flat[0:SC, s * 3 * L:(s + 1) * 3 * L].rearrange("p (c t) -> p c t", c=3) for s in range(GB)]
        eb = wdt[:, :, :].rearrange("p s d -> p (s d)")
        router = h_flat[0:L, GB * 3 * L:]
        e_r, rest, w_r = ([router[:, (3 * s + k) * E:(3 * s + k + 1) * E] for s in range(GB)] for k in range(3))
        rT = [ssm_t[0:E, s * L:(s + 1) * L] for s in range(GB)]

        Y = [bank(f"y{b}") for b in range(GB)]
        BB = bank("b")
        DB = [bank(f"drive{k}") for k in range(2)]
        ACC = bank("acc")
        TB = Y + [ACC, DB[1]]
        OB = [BB, DB[0]]

        const_in = sem("const_in")
        ident_ok = sem("ident_ok")
        x_in = [sem(f"x_in{s}") for s in range(4)]
        a_exp = sem("a_exp")
        a_ready = sem("a_ready")
        ln_chain = sem("ln_chain")
        mv_ready = sem("mv_ready")
        lv_ready = sem("lv_ready")
        rstd_ready = sem("rstd_ready")
        xn_ready = sem("xn_ready")
        lnT_full = sem("lnT_full")
        lnT_used = sem("lnT_used")
        wf_in = [sem(f"wf_in{s}") for s in range(4)]
        xf_full = sem("xf_full")
        conv_started = sem("conv_started")
        conv_chain = sem("conv_chain")
        raw_copied = sem("raw_copied")
        x_silu = sem("x_silu")
        w_in_sem = [sem(f"w_in{s}") for s in range(2)]
        w_used = sem("w_used")
        wdt_in = [sem(f"wdt_in{s}") for s in range(2)]
        misc_full = sem("misc_full")
        ssm_chain = sem("ssm_chain")
        ssm_rows = sem("ssm_rows")
        sq_ready = sem("sq_ready")
        ms_ready = sem("ms_ready")
        ms_log = sem("ms_log")
        rs_ready = sem("rs_ready")
        nrm_ready = sem("nrm_ready")
        bc_stored = sem("bc_stored")
        b_in = [sem(f"b_in{s}") for s in range(2)]
        c_in = [sem(f"c_in{k}") for k in range(4)]
        abs_done = sem("abs_done")
        lin_done = sem("lin_done")
        soft_exp = sem("soft_exp")
        soft_done = sem("soft_done")
        dt_ready = sem("dt_ready")
        u_ready = sem("u_ready")
        zero_cols = sem("zero_cols")
        decay_ready = sem("decay_ready")
        b_full = sem("b_full")
        drive_done = sem("drive_done")
        scan_done = sem("scan_done")
        hc_done = sem("hc_done")
        yT_done = sem("yT_done")
        y_out = sem("y_out")
        gate_raw = sem("gate_raw")
        gate_silu = sem("gate_silu")
        y_skip = sem("y_skip")
        y_ready = sem("y_ready")
        y_copied = sem("y_copied")
        o_copied = sem("o_copied")
        o_added = sem("o_added")
        o_cols = sem("o_cols")
        t_x = [sem(f"t_x{s}") for s in range(GB)]
        t_kT = [sem(f"t_kT{s}") for s in range(2)]
        t_kv = [sem(f"t_kv{s}") for s in range(2)]
        t_out = [sem(f"t_out{s}") for s in range(GB)]
        tail_full = sem("tail_full")
        tail_chain = sem("tail_chain")
        x1_added = sem("x1_added")
        mv1, lv1, rs1, xn1 = (sem(f"tail_{n}1") for n in ("mv", "lv", "rs", "xn"))
        q1_ready = sem("q1_ready")
        max_ready = sem("max_ready")
        e_ready = sem("e_ready")
        eT_ready = sem("eT_ready")
        x2_added = sem("x2_added")
        mv2, lv2, rs2, xn2 = (sem(f"tail_{n}2") for n in ("mv", "lv", "rs", "xn"))
        q2_ready = sem("q2_ready")
        rmax_ready = sem("rmax_ready")
        er_ready = sem("er_ready")
        wr_ready = sem("wr_ready")
        wsum_ready = sem("wsum_ready")
        wT_ready = sem("wT_ready")
        x3_ready = sem("x3_ready")
        mixed = sem("mixed")

        TAIL_READ = {"out": (x1_added, 2), "xT1": (q1_ready, 2), "scores": (e_ready, 1), "eT": (eT_ready, 1),
                     "pv": (x2_added, 2), "xT2": (q2_ready, 2), "logits": (er_ready, 1), "wT": (wT_ready, 1),
                     "mix": (mixed, 2)}

        def read_of(what):
            kind, g, i = what[0], what[1], what[-1]
            it = NQ * g + what[2] if len(what) == 4 else 0
            return {"x": (raw_copied, i + 1), "gate": (gate_raw, NI * g + i + 1), "out": (o_copied, i + 1),
                    "y": (y_copied, QI * it + i + 1) if it < G * NQ - 1 else (y_skip, QI * it + i + 1),
                    "dt": (lin_done, QI * it + i + 1), "ssm": (ssm_rows, 2 * g + 1),
                    "ssm_tokens": (ssm_chain, 7 * g + 1), "ssm_back": (ssm_rows, 2 * g + 2)}[kind]

        def source(n):
            kind, g, i = RING[n]
            return {"x": w_in[i, :, :], "gate": w_in[(NI + i) % (2 * NI), :, :], "out": w_out[i, :, :],
                    "W_x": w_x[i % 2, :, :]}[kind]

        block = stack.enter_context(nc.Block())

        @block.sync
        def _(sp):
            def load_x(b):
                sp.dma_start(xt0[b % 4], x[b, :, :]).then_inc(x_in[b % 4], 16)

            def load_first(i):
                sp.dma_start(w_first[:, i % 4, :], w_in[i, :, :]).then_inc(wf_in[i % 4], 16)

            def load_weights(n, weights):
                if n >= 2:
                    sp.wait_ge(w_used, n - 1)
                sp.dma_start(wr[:, n % 2, 0:weights.shape[1]], weights).then_inc(w_in_sem[n % 2], 16)

            def load_wdt(it):
                if it >= 2:
                    sp.wait_ge(misc_full, MISC[("dt", (it - 2) // NQ, (it - 2) % NQ, QI - 1)] + 1)
                dq = it % NQ
                sp.dma_start(wdt[:, it % 2, :], w_dt[:, dq * QD:(dq + 1) * QD]).then_inc(wdt_in[it % 2], 16)

            def load_b(state):
                if state >= 2:
                    sp.wait_ge(b_full, state - 1)
                sp.dma_start(b_ring[:, state % 2, :],
                             bc_rows[state // (NQ * NS), state % NS, :].partition_broadcast(P))\
                  .then_inc(b_in[state % 2], 16)

            for b in range(GB):
                load_x(b)
            for t, src in ((cw[:, :, :], conv_w), (cb[:, :], conv_b), (a_neg[:, :, :], a_log)):
                sp.dma_start(t, src).then_inc(const_in, 16)
            for i in range(4):
                load_first(i)
            for t, src in ((bdt[:, :], b_dt), (dsk[:, :], d_skip), (rb[:, :], b_router)):
                sp.dma_start(t, src).then_inc(const_in, 16)
            for n in range(2):
                load_weights(n, source(n))
            load_wdt(0)
            load_wdt(1)
            for b in range(GB, B):
                sp.wait_ge(xn_ready, b - GB + 1)
                load_x(b)
            for i in range(4, NI):
                sp.wait_ge(xf_full, i - 3)
                load_first(i)
            def store_bc(g):
                sp.wait_ge(ssm_rows, 2 * g + 2)
                sp.dma_start(bc_rows[g, :, :], ssm_t[R:SSM, :]).then_inc(bc_stored, 16)
                sp.wait_ge(bc_stored, 16 * (g + 1))

            def load_c(g, k):
                if g:
                    sp.wait_ge(hc_done, (NQ - 1) * STEPS + 4 * (k + 1) * GB)
                part = bc_rows[g, NS + 4 * k:NS + 4 * k + 4, :].rearrange("n t -> (n t)")
                sp.dma_start(c_region[:, 4 * k * GT:4 * (k + 1) * GT],
                             part.partition_broadcast(P)).then_inc(c_in[k], 16)

            for n in (2, 3):
                load_weights(n, source(n))
            store_bc(0)
            load_b(0)
            load_b(1)
            for k in range(4):
                load_c(0, k)
                load_weights(4 + k, source(4 + k))
            ring = 2 + EARLY + 2
            for it in range(G * NQ):
                for n in range(NS):
                    if n == 0 and 1 <= it < G * NQ - 1:
                        load_wdt(it + 1)
                    if it == NQ - 1 and n == 10:
                        store_bc(1)
                    if it * NS + n + 2 < G * NQ * NS:
                        load_b(it * NS + n + 2)
                    if it == NQ - 1 and n in (11, 12, 13):
                        load_c(1, n - 11)
                    if it == NQ and n == 0:
                        load_c(1, 3)
                    for step in range(it * STEPS + n * GB, it * STEPS + (n + 1) * GB):
                        for what in FROM_PE.get(step, []):
                            for _ in range({"x": 1, "gate": 1, "out": 1, "ssm": 2}.get(what[0], 0)):
                                if ring < len(RING):
                                    load_weights(ring, source(ring))
                                    ring += 1
            while ring < len(RING):
                load_weights(ring, source(ring))
                ring += 1

            def load_kT(b):
                if b >= 2:
                    sp.wait_ge(tail_full, TAIL_AT[("scores", b - 2, 0)] + 1)
                sp.dma_start(kT[:, b % 2, :, :], ctx_t[b, :, :, :]).then_inc(t_kT[b % 2], 16)

            def load_kv(b):
                if b >= 2:
                    sp.wait_ge(tail_full, TAIL_AT[("pv", b - 2, 1)] + 1)
                sp.dma_start(kv[:, b % 2, :, :], ctx[b, :, :].rearrange("(c p) n -> p c n", p=SC))\
                  .then_inc(t_kv[b % 2], 16)

            def load_rows(b):
                sp.dma_start(xt[b % GB], x[b, :, :]).then_inc(t_x[b % GB], 16)

            sp.wait_ge(w_used, len(RING))
            for b in range(GB):
                load_rows(b)
            n0 = len(RING)
            for j in range(2):
                load_weights(n0 + j, w_out[j, :, :])
            sp.wait_ge(hc_done, 2 * NQ * STEPS)
            sp.dma_start(rw, w_router).then_inc(const_in, 16)
            sp.dma_start(eb[0:E, :], e_bias).then_inc(const_in, 16)
            for b in range(2):
                load_kT(b)
                load_kv(b)
            for j in range(2, 2 * NK):
                load_weights(n0 + j, w_out[j, :, :])
                if j in (5, 9, 11):
                    what, b0 = {5: (load_kT, 2), 9: (load_kv, 2), 11: (load_kT, 4)}[j]
                    what(b0)
                    what(b0 + 1)
            load_kv(4)
            load_kv(5)
            for b in range(GB):
                sp.wait_ge(mixed, 2 * b + 2)
                sp.dma_start(out[b, :, :], xt[b]).then_inc(t_out[b], 16)
            for b in range(GB):
                sp.wait_ge(t_out[b], 16)
                load_rows(GB + b)
            for b in (6, 7):
                load_kT(b)
            for b in (6, 7):
                load_kv(b)
            for b in range(GB, B):
                sp.wait_ge(mixed, 2 * b + 2)
                sp.dma_start(out[b, :, :], xt[b % GB]).then_inc(t_out[b % GB], 16)
            for s in range(GB):
                sp.wait_ge(t_out[s], 32)

        @block.gpsimd
        def _(pool):
            pool.memset(ident[:, :], 0.0).then_inc(ident_ok, 1)
            pool.memset(ones[:, :], 1.0)
            pool.memset(eps_ln[:, :], LN_EPS).then_inc(ident_ok, 1)
            pool.wait_ge(ident_ok, 2)
            pool.affine_select(out=ident[:, :], in_=ident[:, :], compare_op=ALU.not_equal, fill=1.0, base=0,
                               pattern=[[-1, P]], channel_multiplier=1).then_inc(ident_ok, 1)
            pool.wait_ge(xf_full, NI)
            pool.memset(decay[:, :, :, :, 0:1].rearrange("p s b i t -> p (s b i) t"), 0.0).then_inc(zero_cols, 1)

            def dt_times_x(it, i):
                g, dq = it // NQ, it % NQ
                pool.wait_ge(dt_ready, QI * it + i + 1)
                if it >= 2:
                    pool.wait_ge(drive_done, (it - 1) * STEPS)
                pool.tensor_tensor(u[:, it % 2, i, :], dt[:, it % 2, i, :], xs[:, g, QI * dq + i, :],
                                   ALU.mult).then_inc(u_ready, 1)

            def y_gate(it, i):
                g, dq = it // NQ, it % NQ
                pool.wait_ge(y_skip, QI * it + i + 1)
                pool.wait_ge(gate_silu, 2 * it + i // 2 + 1)
                col = xs[:, g, QI * dq + i, :]
                pool.tensor_tensor(col, col, gate[:, i, :], ALU.mult).then_inc(y_ready, 1)

            for it in range(G * NQ):
                g, dq = it // NQ, it % NQ
                for n in range(NS):
                    if dq == 0 and n % 4 == 0:
                        pool.wait_ge(c_in[n // 4], 16 * (g + 1))
                    for b in range(GB):
                        q = n * GB + b
                        if it and q in y_steps(it):
                            y_gate(it - 1, y_steps(it).index(q))
                        if it < G * NQ - 1 and q in u_steps(it) and u_steps(it).index(q) not in U_PAIRS:
                            dt_times_x(it + 1, u_steps(it).index(q))
                        pool.wait_ge(scan_done, it * STEPS + q + 1)
                        c_n = c_bc[:, n, b * L:(b + 1) * L].unsqueeze(1).to_broadcast([P, QI, L])
                        hc = h[:, (it * STEPS + q) % HS, :, :]
                        pool.tensor_tensor(hc, hc, c_n, ALU.mult).then_inc(hc_done, 1)
            for i in range(QI):
                y_gate(G * NQ - 1, i)

        @block.scalar
        def _(act):
            def norm_scale(s, count, mv, lv, rs):
                act.wait_ge(mv, count)
                act.activation(stats[:, s, 14:15], stats[:, s, 13:14], ACT.Ln, bias=eps_ln[0:L, :]).then_inc(lv, 1)
                act.wait_ge(lv, count)
                act.activation(stats[:, s, 15:16], stats[:, s, 14:15], ACT.Exp, scale=-0.5).then_inc(rs, 1)

            def conv_start(psum, i, g):
                act.activation(xs[:, g, i, :], psum[:, 0:GT], ACT.Identity,
                               bias=cb[:, i:i + 1], scale=cw[:, i, KC - 1:KC]).then_inc(conv_started, 1)

            def norm_columns(b):
                for half in range(2):
                    act.wait_ge(lnT_full, 2 * b + half + 1)
                    act.copy(xnT[:, 4 * half:4 * half + 4, b * L:(b + 1) * L],
                             Y[2 + half][:, 0:4 * L].rearrange("p (k t) -> p k t", k=4)).then_inc(lnT_used, 1)

            act.preload_act_table_set(LOG_EXP)
            act.wait_ge(ident_ok, 3)
            norm_scale(0, 1, mv_ready, lv_ready, rstd_ready)
            for b in range(GB):
                if b < GB - 1:
                    norm_scale(b + 1, b + 2, mv_ready, lv_ready, rstd_ready)
                norm_columns(b)
            act.wait_ge(const_in, 16 * 6)
            act.activation(a_neg[:, :, :], a_neg[:, :, :], ACT.Exp).then_inc(a_exp, 1)
            for i in range(NI):
                if i < GB:
                    norm_scale(i, GB + i + 1, mv_ready, lv_ready, rstd_ready)
                act.wait_ge(xf_full, i + 1)
                conv_start(Y[i % 2], i, 0)
                if i < GB:
                    norm_columns(GB + i)
                else:
                    done = range(GB) if i == GB else range(i - 1, i)
                    act.wait_ge(conv_chain, 3 * i)
                    part = xs[:, 0, done[0]:i, :]
                    act.activation(part, part, ACT.Silu).then_inc(x_silu, len(done))
            act.wait_ge(conv_chain, 3 * NI)
            part = xs[:, 0, NI - 1, :]
            act.activation(part, part, ACT.Silu).then_inc(x_silu, 1)
            act.preload_act_table_set(LOG_EXP)

            def ssm_copy(g, back=False):
                what = ("ssm_back" if back else "ssm", g)
                act.wait_ge(misc_full, MISC[what] + 1)
                act.copy(ssm_t[:, :], (ACC if g else DB[job_bank(what)])[0:SSM, 0:GT]).then_inc(ssm_rows, 1)

            def ssm_square(g):
                act.wait_ge(ssm_chain, 7 * g + 1)
                act.activation(tok_sq, tok, ACT.Square).then_inc(sq_ready, 1)

            def ssm_scale(g):
                act.wait_ge(ms_ready, g + 1)
                act.activation(ms[:, :, :], ms[:, :, :], ACT.Ln).then_inc(ms_log, 1)
                act.wait_ge(ms_log, g + 1)
                act.activation(ms[:, :, :], ms[:, :, :], ACT.Exp, scale=-0.5).then_inc(rs_ready, 1)

            def soft_start(it, i):
                g, dq = it // NQ, it % NQ
                what = ("dt", g, dq, i)
                act.wait_ge(misc_full, MISC[what] + 1)
                act.activation(lin[:, i, :], (ACC if it else DB[job_bank(what)])[:, 0:GT], ACT.Identity,
                               bias=bdt[:, QI * dq + i:QI * dq + i + 1]).then_inc(lin_done, 1)

            def soft_abs(it, i=slice(None), count=QI):
                act.wait_ge(lin_done, QI * (it + 1))
                if it >= 2:
                    act.wait_ge(u_ready, QI * (it - 1))
                act.activation(dt[:, it % 2, i, :], lin[:, i, :], ACT.Abs).then_inc(abs_done, count)

            def soft_exp_abs(it, i=slice(None), first=0, count=QI):
                d = dt[:, it % 2, i, :]
                act.wait_ge(abs_done, QI * it + first + count)
                act.activation(d, d, ACT.Exp, scale=-1.0).then_inc(soft_exp, count)

            def soft_log(it, i=slice(None), first=0, count=QI):
                d = dt[:, it % 2, i, :]
                act.wait_ge(soft_exp, QI * it + first + count)
                act.activation(d, d, ACT.Ln, bias=1.0).then_inc(soft_done, count)

            def decay_tile(it, n, i):
                state = it * NS + n
                act.wait_ge(dt_ready, QI * it + i + 1)
                if i == 0:
                    if state >= 2:
                        act.wait_ge(scan_done, GB * (state - 1))
                tile = QI * (it % NQ) + i
                a = act.activation(decay[:, state % 2, :, i, 1:L],
                                   dt[:, it % 2, i, :].rearrange("p (b t) -> p b t", b=GB)[:, :, 1:L],
                                   ACT.Exp, scale=a_neg[:, tile, n:n + 1])
                if i == QI - 1:
                    a.then_inc(decay_ready, 1)

            def b_copy(state):
                act.wait_ge(b_in[state % 2], 16 * (state // 2 + 1))
                if state:
                    act.wait_ge(drive_done, GB * state)
                act.copy(BB[:, 0:GT], b_ring[:, state % 2, :]).then_inc(b_full, 1)

            def x_silus(first, last):
                act.wait_ge(conv_chain, 3 * (NI + last))
                part = xs[:, 1, first:last, :]
                act.activation(part, part, ACT.Silu).then_inc(x_silu, last - first)

            def silus(it, part):
                act.wait_ge(gate_raw, QI * it + 2 * part + 2)
                pair = gate[:, 2 * part:2 * part + 2, :]
                act.activation(pair, pair, ACT.Silu).then_inc(gate_silu, 1)
                if part == 0:
                    return
                if it < NQ - 1:
                    x_silus(EARLY + QI * it if it else 0, EARLY + QI * (it + 1))
                act.preload_act_table_set(LOG_EXP)

            def y_rows(it):
                act.wait_ge(dt_ready, QI * (it + 1))
                for b in range(GB):
                    act.wait_ge(yT_done, (it + 1) * STEPS - GB + b + 1)
                    act.copy(y_t[:, b, :], Y[b][0:L, :]).then_inc(y_out, 1)

            def projected(what):
                kind, g, i = what
                act.wait_ge(w_used, WEIGHT_USE[what] + 1)
                if kind == "gate":
                    n = NI * g + i
                    if n >= QI:
                        act.wait_ge(y_ready, n - QI + 1)
                    act.copy(gate[:, i % QI, :], ACC[:, 0:GT]).then_inc(gate_raw, 1)
                elif kind == "x":
                    act.wait_ge(conv_chain, 3 * (NI + i))
                    act.copy(raw[:, :], ACC[:, 0:GT]).then_inc(raw_copied, 1)
                    act.wait_ge(raw_copied, i + 1)
                    conv_start(raw, i, 1)
                elif i % 2 == 0:
                    act.copy(xnT[:, i // 2, 0:GT], ACC[:, 0:GT]).then_inc(o_copied, 1)
                else:
                    act.wait_ge(o_added, i // 2)
                    act.wait_ge(conv_chain, 6 * NI)
                    act.copy(raw[:, :], ACC[:, 0:GT]).then_inc(o_copied, 1)

            def y_copy(it, i):
                g = it // NQ
                act.wait_ge(misc_full, MISC[("y", g, it % NQ, i)] + 1)
                if i >= 2:
                    act.wait_ge(y_skip, QI * it + i - 1)
                elif it:
                    act.wait_ge(y_skip, QI * it)
                act.copy(y_side[:, i % 2, :], ACC[:, 0:GT]).then_inc(y_copied, 1)

            def from_pe(step):
                for what in FROM_PE.get(step, []):
                    if what[0] == "y":
                        y_copy(NQ * what[1] + what[2], what[3])
                    elif what[0] == "dt":
                        soft_start(NQ * what[1] + what[2], what[3])
                    elif what[0] in ("ssm", "ssm_back"):
                        ssm_copy(1, what[0] == "ssm_back")
                    elif what[0] != "ssm_tokens":
                        projected(what)

            ssm_copy(0)
            ssm_square(0)
            ssm_scale(0)
            projected(("x", 0, 0))
            ssm_copy(0, back=True)
            for i in range(QI):
                soft_start(0, i)
            for i in range(QI):
                soft_abs(0, i, 1)
            for i in range(QI):
                soft_exp_abs(0, i, i, 1)
            projected(("x", 0, 1))
            for i in range(QI):
                soft_log(0, i, i, 1)
            b_copy(0)
            act.wait_ge(zero_cols, 1)
            act.wait_ge(a_ready, 1)
            for i in range(QI):
                decay_tile(0, 0, i)
            projected(("x", 0, 2))
            last = G * NQ - 1
            for it in range(G * NQ):
                for n in range(NS):
                    step = it * STEPS + n * GB
                    more = n < NS - 1 or it < last
                    from_pe(step)
                    for i in range(QI):
                        if more:
                            decay_tile(it + (n + 1) // NS, (n + 1) % NS, i)
                        if i == 1:
                            from_pe(step + 1)
                    if it == 0 and n == 0:
                        projected(("x", 0, EARLY - 1))
                    from_pe(step + 2)
                    if it and n == silu_at(it):
                        silus(it - 1, 0)
                    if more:
                        b_copy(it * NS + n + 1)
                    from_pe(step + 3)
                    if it and n == silu_at(it):
                        silus(it - 1, 1)
                    if it == NQ - 1 and n == 7:
                        ssm_square(1)
                        ssm_scale(1)
                    if it < last and n == soft_at(it):
                        soft_abs(it + 1)
                    if it < last and n == soft_at(it) + 1:
                        soft_exp_abs(it + 1)
                    if it < last and n == soft_at(it) + 2:
                        soft_log(it + 1)
                    if n == 0 and it:
                        y_rows(it - 1)
            for step in range(G * NQ * STEPS, G * NQ * STEPS + AFTER):
                from_pe(step)
            y_rows(last)
            silus(last, 0)
            silus(last, 1)
            for i in range(LATE):
                projected(("out", 1, NI - LATE + i))

            def out_columns(ho):
                act.wait_ge(w_used, len(RING) + 2 * (ho + 1))
                act.copy(xnT[:, ho, GT:2 * GT], OB[ho % 2][:, 0:GT]).then_inc(o_cols, 1)

            def columns(what, b, ready):
                for half in range(2):
                    n = TAIL_AT[(what, b, half)]
                    act.wait_ge(tail_full, n + 1)
                    act.copy(q_b[b % GB][:, 4 * half:4 * half + 4, :],
                             TB[n % 6][:, 0:4 * L].rearrange("p (k t) -> p k t", k=4)).then_inc(ready, 1)

            for g in range(G):
                batches = range(GB * g, GB * (g + 1))
                fill = (lambda k: out_columns(k)) if g == 0 else (lambda k: None)
                fill(0)
                for b in batches:
                    norm_scale(b % GB, b + 1, mv1, lv1, rs1)
                for b in batches:
                    columns("xT1", b, q1_ready)
                fill(1)
                for b in batches:
                    n = TAIL_AT[("scores", b, 0)]
                    act.wait_ge(max_ready, b + 1)
                    act.activation(e_b[b % GB], TB[n % 6][0:L, 0:SK], ACT.Exp, bias=sm[:, b % GB, 0:1],
                                   accum_out=sm[:, b % GB, 1:2]).then_inc(e_ready, 1)
                fill(2)
                for b in batches:
                    n = TAIL_AT[("eT", b, 0)]
                    act.wait_ge(tail_full, n + 1)
                    act.copy(eT[b % GB], TB[n % 6][0:SC, 0:3 * L].rearrange("p (c t) -> p c t", c=3))\
                       .then_inc(eT_ready, 1)
                fill(3)
                fill(4)
                for b in batches:
                    norm_scale(b % GB, b + 1, mv2, lv2, rs2)
                for b in batches:
                    columns("xT2", b, q2_ready)
                fill(5)
                for b in batches:
                    n = TAIL_AT[("logits", b, 0)]
                    act.wait_ge(rmax_ready, b + 1)
                    act.activation(e_r[b % GB], TB[n % 6][0:L, 0:E], ACT.Exp, bias=sm[:, b % GB, 3:4],
                                   accum_out=sm[:, b % GB, 4:5]).then_inc(er_ready, 1)
                fill(6)
                for b in batches:
                    n = TAIL_AT[("wT", b, 0)]
                    act.wait_ge(tail_full, n + 1)
                    act.copy(rT[b % GB], TB[n % 6][0:E, 0:L]).then_inc(wT_ready, 1)
                fill(7)

        @block.tensor
        def _(pe):
            def transpose(o, i, last=True, start=True):
                k = i.shape[0]
                return pe.matmul(o, lhsT=i, rhs=ident[0:k, 0:k], start=start, stop=last, is_transpose=True)

            def norm_turn(b):
                pe.wait_ge(xn_ready, b + 1)
                if b:
                    pe.wait_ge(lnT_used, 2 * b)
                for half in range(2):
                    for k in range(4):
                        last = transpose(Y[2 + half][:, k * L:(k + 1) * L],
                                         xn0[b % 3][:, (4 * half + k) * P:(4 * half + k + 1) * P])
                    last.then_inc(lnT_full, 1)

            pe.wait_ge(ident_ok, 3)
            for b in range(GB):
                norm_turn(b)

            def small(what):
                if what in ACC_ORDER:
                    pe.wait_ge(*read_of(ACC_ORDER[ACC_ORDER.index(what) - 1]))
                    return ACC
                m = MISC[what]
                if what[0] == "y" and what[-1] < 2:
                    pe.wait_ge(scan_done, G * NQ * STEPS)
                elif m >= 2:
                    pe.wait_ge(*read_of(list(MISC)[m - 2]))
                return DB[job_bank(what)]

            def ssm_product(g, i):
                bank_ = small(("ssm", g)) if i == 0 else ACC if g else DB[job_bank(("ssm", g))]
                n = WEIGHT_USE[("W_x", g, i // 8)]
                if i % 8 == 0:
                    pe.wait_ge(w_in_sem[n % 2], 16 * (n // 2 + 1))
                pe.wait_ge(x_silu, NI * g + i + 1)
                last = pe.matmul(bank_[0:SSM, 0:GT], lhsT=wr[:, n % 2, (i % 8) * SSM:(i % 8 + 1) * SSM],
                                 rhs=xs[:, g, i, :], start=(i == 0), stop=(i == NI - 1))
                if i == 7:
                    last.then_inc(w_used, 1)
                if i == NI - 1:
                    last.then_inc(misc_full, 1)
                    pe.wait_ge(misc_full, MISC[("ssm", g)] + 1)
                    pe.sem_inc(w_used, 1)

            def ssm_tokens(g):
                bank_ = small(("ssm_tokens", g))
                pe.wait_ge(ssm_rows, 2 * g + 1)
                for b in range(GB):
                    last = transpose(bank_[0:L, b * SSM:(b + 1) * SSM], ssm_t[:, b * L:(b + 1) * L])
                last.then_inc(misc_full, 1)

            def ssm_back(g):
                bank_ = small(("ssm_back", g))
                pe.wait_ge(nrm_ready, g + 1)
                for b in range(GB):
                    last = transpose(bank_[0:SSM, b * L:(b + 1) * L], nrm[:, b, :])
                last.then_inc(misc_full, 1)

            def dt_tile(it, i):
                bank_ = small(("dt", it // NQ, it % NQ, i))
                pe.wait_ge(wdt_in[it % 2], 16 * (it // 2 + 1))
                pe.matmul(bank_[:, 0:GT], lhsT=wdt[:, it % 2, i * P:(i + 1) * P], rhs=ssm_t[0:R, :],
                          start=True, stop=True).then_inc(misc_full, 1)

            def y_tile(it, i):
                bank_ = small(("y", it // NQ, it % NQ, i))
                pe.wait_ge(y_out, GB * (it + 1))
                for b in range(GB):
                    last = transpose(bank_[:, b * L:(b + 1) * L], y_t[:, b, i * P:(i + 1) * P])
                last.then_inc(misc_full, 1)

            def sum_states(step):
                it, n, b = step // STEPS, step % STEPS // GB, step % GB
                pe.wait_ge(hc_done, step + 1)
                if n == 0 and it:
                    pe.wait_ge(y_out, GB * (it - 1) + b + 1)
                for i in range(QI):
                    last = transpose(Y[b][0:L, i * P:(i + 1) * P], h[:, step % HS, i, :],
                                     last=(n == NS - 1 and i == QI - 1), start=(n == 0 and i == 0))
                last.then_inc(yT_done, 1)

            def projection(what, k):
                kind, g, i = what
                n = WEIGHT_USE[what]
                if k == 0:
                    pe.wait_ge(w_in_sem[n % 2], 16 * (n // 2 + 1))
                    if ACC_ORDER.index(what):
                        pe.wait_ge(*read_of(ACC_ORDER[ACC_ORDER.index(what) - 1]))
                if kind == "out":
                    rhs = xs[:, 0, 8 * (i % 2) + k, :]
                else:
                    half = 1 if kind == "x" else g
                    rhs = xnT[:, k, half * GT:(half + 1) * GT]
                last = pe.matmul(ACC[:, 0:GT], lhsT=wr[:, n % 2, k * P:(k + 1) * P], rhs=rhs,
                                 start=(k == 0), stop=(k == NK - 1))
                if k == NK - 1:
                    last.then_inc(w_used, 1)

            def early(j, ks):
                for k in ks:
                    projection(("x", 0, j), k)

            for i in range(NI):
                pe.wait_ge(wf_in[i % 4], 16 * (i // 4 + 1))
                if i == 0:
                    pe.wait_ge(lnT_used, 2 * GB)
                if i >= 2:
                    pe.wait_ge(conv_chain, 3 * (i - 1))
                for k in range(NK):
                    last = pe.matmul(Y[i % 2][:, 0:GT], lhsT=w_first[:, i % 4, k * P:(k + 1) * P],
                                     rhs=xnT[:, k, 0:GT], start=(k == 0), stop=(k == NK - 1))
                last.then_inc(xf_full, 1)
                if i < GB:
                    norm_turn(GB + i)
                if i >= GB + 1:
                    for t in (range(3) if i == GB + 1 else range(i - 3, i - 2) if i < NI - 1 else range(i - 3, i - 1)):
                        ssm_product(0, t)
            pe.wait_ge(lnT_used, 2 * B)
            early(0, range(0, 3))
            ssm_product(0, NI - 2)
            ssm_product(0, NI - 1)
            early(0, range(3, 5))
            ssm_tokens(0)
            early(0, range(5, 8))
            ssm_back(0)
            early(1, range(1))
            pe.wait_ge(ssm_rows, 2)
            for i in range(QI):
                dt_tile(0, i)
            early(1, range(1, 8))
            early(2, range(8))
            early(3, range(8))
            for it in range(G * NQ):
                for q in range(STEPS):
                    step = it * STEPS + q
                    if step >= LAG:
                        sum_states(step - LAG)
                    for what, first, last in PLAN[it]:
                        kind = what[0]
                        if kind in ("x", "out", "gate"):
                            for k, at in enumerate(matmul_steps(first, last, NK)):
                                if at == q:
                                    projection(what, k)
                        elif kind == "ssm":
                            for i, at in enumerate(matmul_steps(first, last, NI)):
                                if at == q:
                                    ssm_product(1, i)
                        elif first == q and kind == "ssm_tokens":
                            ssm_tokens(1)
                        elif first == q and kind == "ssm_back":
                            ssm_back(1)
                        elif first == q:
                            (y_tile if kind == "y" else dt_tile)(NQ * what[1] + what[2], what[3])
            for step in range(G * NQ * STEPS - LAG, G * NQ * STEPS):
                sum_states(step)
            for i in range(LATE):
                for k in range(NK):
                    projection(("out", 1, NI - LATE + i), k)
                if i == 0:
                    for t in range(QI):
                        y_tile(NQ * G - 1, t)

            def output_tile(ho):
                if ho >= 2:
                    pe.wait_ge(o_cols, ho - 1)
                for hf in range(2):
                    n = len(RING) + 2 * ho + hf
                    pe.wait_ge(w_in_sem[n % 2], 16 * (n // 2 + 1))
                    for k in range(8):
                        last = pe.matmul(OB[ho % 2][:, 0:GT], lhsT=wr[:, n % 2, k * P:(k + 1) * P],
                                         rhs=xs[:, 1, 8 * hf + k, :], start=(hf == 0 and k == 0),
                                         stop=(hf == 1 and k == 7))
                    last.then_inc(w_used, 1)

            def tail_bank(what, b, part=0):
                n = TAIL_AT[(what, b, part)]
                if n >= 6:
                    w, bb, k = TAIL[n - 6]
                    read, parts = TAIL_READ[w]
                    pe.wait_ge(read, parts * bb + k + 1)
                return TB[n % 6]

            def turn_rows(what, b, ready):
                pe.wait_ge(ready, b + 1)
                for half in range(2):
                    bank_ = tail_bank(what, b, half)
                    for k in range(4):
                        last = transpose(bank_[:, k * L:(k + 1) * L],
                                         xn[b % GB][:, (4 * half + k) * P:(4 * half + k + 1) * P])
                    last.then_inc(tail_full, 1)

            pe.wait_ge(y_ready, 2 * NQ * QI)
            for g in range(G):
                batches = range(GB * g, GB * (g + 1))
                fill = (lambda k: output_tile(k)) if g == 0 else (lambda k: None)
                pe.wait_ge(*((o_cols, NK) if g else (o_added, NK)))
                for b in batches:
                    for half in range(2):
                        bank_ = tail_bank("out", b, half)
                        for k in range(4):
                            last = transpose(bank_[0:L, k * P:(k + 1) * P], xnT[:, 4 * half + k, b * L:(b + 1) * L])
                        last.then_inc(tail_full, 1)
                fill(0)
                for b in batches:
                    turn_rows("xT1", b, xn1)
                fill(1)
                for b in batches:
                    bank_ = tail_bank("scores", b)
                    pe.wait_ge(q1_ready, 2 * b + 2)
                    pe.wait_ge(t_kT[b % 2], 16 * (b // 2 + 1))
                    for k in range(NK):
                        last = pe.matmul(bank_[0:L, 0:SK], lhsT=q_b[b % GB][:, k, :], rhs=kT[:, b % 2, k, :],
                                         start=(k == 0), stop=(k == NK - 1))
                    last.then_inc(tail_full, 1)
                fill(2)
                for b in batches:
                    bank_ = tail_bank("eT", b)
                    pe.wait_ge(e_ready, b + 1)
                    for k in range(3):
                        last = transpose(bank_[0:SC, k * L:(k + 1) * L], e_b[b % GB][:, k * SC:(k + 1) * SC])
                    last.then_inc(tail_full, 1)
                fill(3)
                for b in batches:
                    pe.wait_ge(eT_ready, b + 1)
                    pe.wait_ge(t_kv[b % 2], 16 * (b // 2 + 1))
                    for half in range(2):
                        bank_ = tail_bank("pv", b, half)
                        for k in range(3):
                            last = pe.matmul(bank_[0:L, :], lhsT=eT[b % GB][:, k, :],
                                             rhs=kv[:, b % 2, k, half * 512:(half + 1) * 512],
                                             start=(k == 0), stop=(k == 2))
                        last.then_inc(tail_full, 1)
                fill(4)
                for b in batches:
                    turn_rows("xT2", b, xn2)
                fill(5)
                if g == 0:
                    pe.wait_ge(const_in, 16 * 8)
                for b in batches:
                    bank_ = tail_bank("logits", b)
                    pe.wait_ge(q2_ready, 2 * b + 2)
                    for k in range(NK):
                        pe.matmul(bank_[0:L, 0:E], lhsT=q_b[b % GB][:, k, :], rhs=rw[:, k, :],
                                  start=(k == 0), stop=False)
                    pe.matmul(bank_[0:L, 0:E], lhsT=ones[:, :], rhs=rb[:, :], start=False, stop=True)\
                      .then_inc(tail_full, 1)
                fill(6)
                for b in batches:
                    bank_ = tail_bank("wT", b)
                    pe.wait_ge(wr_ready, b + 1)
                    transpose(bank_[0:E, 0:L], w_r[b % GB]).then_inc(tail_full, 1)
                for b in batches:
                    pe.wait_ge(wT_ready, b + 1)
                    for half in range(2):
                        bank_ = tail_bank("mix", b, half)
                        pe.matmul(bank_[0:L, :], lhsT=rT[b % GB], rhs=eb[0:E, half * 512:(half + 1) * 512],
                                  start=True, stop=True).then_inc(tail_full, 1)
                fill(7)

        @block.vector
        def _(dve):
            def link(ins, chain, count):
                count[0] += 1
                ins.then_inc(chain, 1)
                dve.wait_ge(chain, count[0])

            ln_count = [0]
            conv_count = [0]
            tail_count = [0]

            def norm_stats(rows, s, ready, chain, count):
                for half in range(2):
                    dve.bn_stats(stats[:, s, 6 * half:6 * half + 6],
                                 rows[:, half * 512:(half + 1) * 512]).then_inc(chain, 1)
                count[0] += 2
                dve.wait_ge(chain, count[0])
                dve.bn_aggr(stats[:, s, 12:14], stats[:, s, 0:12]).then_inc(ready, 1)

            def norm_apply(normed, rows, s, count, rs, ready):
                dve.wait_ge(rs, count)
                dve.tensor_scalar(normed, rows, stats[:, s, 12:13], stats[:, s, 15:16],
                                  ALU.subtract, ALU.mult).then_inc(ready, 1)

            def row_stats(b):
                s = b % 4
                dve.wait_ge(x_in[s], 16 * (b // 4 + 1))
                if b >= 4:
                    dve.wait_ge(xn_ready, b - 3)
                norm_stats(xt0[s], s, mv_ready, ln_chain, ln_count)

            def row_apply(b):
                if b >= 3:
                    dve.wait_ge(lnT_full, 2 * (b - 2))
                norm_apply(xn0[b % 3], xt0[b % 4], b % 4, b + 1, rstd_ready, xn_ready)

            def conv(psum, i, g):
                dve.wait_ge(conv_started, NI * g + i + 1)
                col = xs[:, g, i, :].rearrange("p (b t) -> p b t", b=GB)
                raw = psum[:, 0:GT].rearrange("p (b t) -> p b t", b=GB)
                for back in range(1, KC):
                    ins = dve.scalar_tensor_tensor(col[:, :, back:L], raw[:, :, 0:L - back],
                                                   cw[:, i, KC - 1 - back:KC - back], col[:, :, back:L],
                                                   ALU.mult, ALU.add)
                    link(ins, conv_chain, conv_count)

            row_stats(0)
            for b in range(GB):
                if b < GB - 1:
                    row_stats(b + 1)
                row_apply(b)
            for i in range(NI):
                if i < GB:
                    row_stats(GB + i)
                    row_apply(GB + i)
                conv(Y[i % 2], i, 0)
            dve.wait_ge(a_exp, 1)
            dve.tensor_scalar(a_neg[:, :, :], a_neg[:, :, :], -1.0, None, ALU.mult).then_inc(a_ready, 1)

            ssm_count = [0]
            parts = ((0, R), (R, R + NS), (R + NS, SSM))

            def ssm_rows_copy(g):
                dve.wait_ge(misc_full, MISC[("ssm_tokens", g)] + 1)
                tokens = (ACC if g else DB[1])[0:L, 0:GB * SSM]
                dve.tensor_copy(tok, tokens.rearrange("p (b d) -> p b d", b=GB)).then_inc(ssm_chain, 1)
                ssm_count[0] += 1

            def ssm_means(g):
                dve.wait_ge(sq_ready, g + 1)
                for k, (a, z) in enumerate(parts):
                    link(dve.reduce_sum(ms[:, k, :], tok_sq[:, :, a:z], AX.X), ssm_chain, ssm_count)
                link(dve.tensor_scalar(ms[:, 0, :], ms[:, 0, :], 1.0 / R, RMS_EPS, ALU.mult, ALU.add),
                     ssm_chain, ssm_count)
                dve.tensor_scalar(ms[:, 1:3, :], ms[:, 1:3, :], 1.0 / NS, RMS_EPS, ALU.mult, ALU.add)\
                   .then_inc(ms_ready, 1)

            def ssm_divide(g):
                dve.wait_ge(rs_ready, g + 1)
                for k, (a, z) in enumerate(parts):
                    ins = dve.tensor_tensor(nrm[:, :, a:z], tok[:, :, a:z],
                                            ms[:, k, :].unsqueeze(2).to_broadcast([L, GB, z - a]), ALU.mult)
                    if k < 2:
                        link(ins, ssm_chain, ssm_count)
                ins.then_inc(nrm_ready, 1)

            def soft_add(it, i):
                dve.wait_ge(soft_done, QI * it + i + 1)
                d = dt[:, it % 2, i, :]
                dve.scalar_tensor_tensor(d, lin[:, i, :], 0.0, d, ALU.max, ALU.add).then_inc(dt_ready, 1)

            def y_tile(it, i):
                g, dq = it // NQ, it % NQ
                tile = QI * dq + i
                col = xs[:, g, tile, :]
                if it < G * NQ - 1:
                    dve.wait_ge(y_copied, QI * it + i + 1)
                    y = y_side[:, i % 2, :]
                else:
                    dve.wait_ge(misc_full, MISC[("y", g, dq, i)] + 1)
                    y = DB[job_bank(("y", g, dq, i))][:, 0:GT]
                dve.scalar_tensor_tensor(col, col, dsk[:, tile:tile + 1], y, ALU.mult, ALU.add).then_inc(y_skip, 1)

            def output_add(ho):
                dve.wait_ge(o_copied, 2 * ho + 2)
                col = xnT[:, ho, 0:GT]
                dve.tensor_tensor(col, col, raw[:, :], ALU.add).then_inc(o_added, 1)

            def dt_times_x(it, i):
                g, dq = it // NQ, it % NQ
                dve.wait_ge(dt_ready, QI * it + i + 1)
                if it >= 2:
                    dve.wait_ge(drive_done, (it - 1) * STEPS)
                dve.tensor_tensor(u[:, it % 2, i, :], dt[:, it % 2, i, :], xs[:, g, QI * dq + i, :],
                                  ALU.mult).then_inc(u_ready, 1)

            def drive(it, n, b):
                step = it * STEPS + n * GB + b
                if b == 0:
                    dve.wait_ge(b_full, it * NS + n + 1)
                if step >= 2:
                    dve.wait_ge(scan_done, step - 1)
                b_n = BB[:, b * L:(b + 1) * L].unsqueeze(1).to_broadcast([P, QI, L])
                dve.tensor_tensor(DB[b % 2][:, 0:QI * L].rearrange("p (i t) -> p i t", i=QI),
                                  u[:, it % 2, :, b * L:(b + 1) * L], b_n, ALU.mult).then_inc(drive_done, 1)

            def scan(it, n, b):
                step = it * STEPS + n * GB + b
                if b == 0:
                    dve.wait_ge(decay_ready, it * NS + n + 1)
                if step >= HS:
                    dve.wait_ge(yT_done, step - HS + 1)
                dve.wait_ge(drive_done, step + 1)
                dve.tensor_tensor_scan(h[:, step % HS, :, :].rearrange("p i t -> p (i t)"),
                                       decay[:, (it * NS + n) % 2, b, :, :].rearrange("p i t -> p (i t)"),
                                       DB[b % 2][:, 0:QI * L], 0.0, ALU.mult, ALU.add)\
                   .then_inc(scan_done, 1)

            def tap(i, back, g=1):
                if back == 1:
                    dve.wait_ge(conv_started, NI * g + i + 1)
                else:
                    dve.wait_ge(conv_chain, 3 * (NI * g + i) + back - 1)
                col = xs[:, g, i, :].rearrange("p (b t) -> p b t", b=GB)
                before = raw[:, :].rearrange("p (b t) -> p b t", b=GB)
                dve.scalar_tensor_tensor(col[:, :, back:L], before[:, :, 0:L - back],
                                         cw[:, i, KC - 1 - back:KC - back], col[:, :, back:L],
                                         ALU.mult, ALU.add).then_inc(conv_chain, 1)

            def beside(it, pair):
                if it == 0 and pair < 2:
                    for back in ((1, 2), (3,))[pair]:
                        tap(EARLY - 2, back)
                if it == 0 and 2 <= pair < 2 + KC - 1:
                    tap(EARLY - 1, pair - 1)
                for q, plan in enumerate(PLAN):
                    for (kind, _, *i), _, last in plan:
                        back = it * STEPS // 2 + pair - (q * STEPS + last + AFTER) // 2
                        if kind == "x" and 1 <= back < KC:
                            tap(i[0], back)
                        if kind == "out" and i[0] % 2 and back == 1:
                            output_add(i[0] // 2)
                if it and pair in y_pairs(it):
                    y_tile(it - 1, y_pairs(it).index(pair))
                if it < G * NQ - 1 and pair in soft_pairs(it):
                    soft_add(it + 1, soft_pairs(it).index(pair))
                if it < G * NQ - 1:
                    for i, at in U_PAIRS.items():
                        if pair == at:
                            dt_times_x(it + 1, i)
                if it == NQ - 1 and pair == 13:
                    ssm_rows_copy(1)
                if it == NQ - 1 and pair == 15:
                    ssm_means(1)
                if it == NQ - 1 and pair == 16:
                    ssm_divide(1)

            dve.wait_ge(zero_cols, 1)
            ssm_rows_copy(0)
            ssm_means(0)
            ssm_divide(0)
            for i in range(2):
                for back in range(1, KC):
                    tap(i, back)
            for i in range(QI):
                soft_add(0, i)
            for i in range(QI):
                dt_times_x(0, i)
            for it in range(G * NQ):
                dve.wait_ge(u_ready, QI * (it + 1))
                for n in range(NS):
                    for pair in range(2):
                        for b in (2 * pair, 2 * pair + 1):
                            drive(it, n, b)
                        for b in (2 * pair, 2 * pair + 1):
                            scan(it, n, b)
                        beside(it, 2 * n + pair)
            for i in range(QI):
                y_tile(NQ * G - 1, i)
            output_add(NI // 2 - 1)

            for g in range(G):
                batches = range(GB * g, GB * (g + 1))
                for b in batches:
                    s = b % GB
                    dve.wait_ge(t_x[s], 16 * (g + 1))
                    for half in range(2):
                        n = TAIL_AT[("out", b, half)]
                        part = xt[s][:, half * 512:(half + 1) * 512]
                        dve.wait_ge(tail_full, n + 1)
                        dve.tensor_tensor(part, part, TB[n % 6][0:L, :], ALU.add).then_inc(x1_added, 1)
                    dve.wait_ge(x1_added, 2 * b + 2)
                    norm_stats(xt[s], s, mv1, tail_chain, tail_count)
                for b in batches:
                    norm_apply(xn[b % GB], xt[b % GB], b % GB, b + 1, rs1, xn1)
                for b in batches:
                    n = TAIL_AT[("scores", b, 0)]
                    dve.wait_ge(tail_full, n + 1)
                    dve.reduce_max(sm[:, b % GB, 0:1], TB[n % 6][0:L, 0:SK], AX.X, negate=True).then_inc(max_ready, 1)
                for b in batches:
                    dve.wait_ge(e_ready, b + 1)
                    link(dve.reciprocal(sm[:, b % GB, 2:3], sm[:, b % GB, 1:2]), tail_chain, tail_count)
                for b in batches:
                    s = b % GB
                    for half in range(2):
                        n = TAIL_AT[("pv", b, half)]
                        part = xt[s][:, half * 512:(half + 1) * 512]
                        dve.wait_ge(tail_full, n + 1)
                        dve.scalar_tensor_tensor(part, TB[n % 6][0:L, :], sm[:, s, 2:3], part,
                                                 ALU.mult, ALU.add).then_inc(x2_added, 1)
                    dve.wait_ge(x2_added, 2 * b + 2)
                    norm_stats(xt[s], s, mv2, tail_chain, tail_count)
                for b in batches:
                    norm_apply(xn[b % GB], xt[b % GB], b % GB, b + 1, rs2, xn2)
                for b in batches:
                    n = TAIL_AT[("logits", b, 0)]
                    dve.wait_ge(tail_full, n + 1)
                    dve.reduce_max(sm[:, b % GB, 3:4], TB[n % 6][0:L, 0:E], AX.X, negate=True).then_inc(rmax_ready, 1)
                for b in batches:
                    s = b % GB
                    dve.wait_ge(er_ready, b + 1)
                    link(dve.max(sm[:, s, 8:16], e_r[s]), tail_chain, tail_count)
                    link(dve.match_replace(rest[s], sm[:, s, 8:16], e_r[s], -1.0), tail_chain, tail_count)
                    link(dve.scalar_tensor_tensor(w_r[s], rest[s], 0.0, e_r[s], ALU.max, ALU.subtract),
                         tail_chain, tail_count)
                    link(dve.reciprocal(sm[:, s, 5:6], sm[:, s, 4:5]), tail_chain, tail_count)
                    dve.tensor_scalar(w_r[s], w_r[s], sm[:, s, 5:6], -1.0, ALU.mult, ALU.mult).then_inc(wr_ready, 1)
                for b in batches:
                    s = b % GB
                    dve.wait_ge(wr_ready, b + 1)
                    dve.reduce_sum(sm[:, s, 6:7], w_r[s], AX.X).then_inc(wsum_ready, 1)
                    dve.wait_ge(wsum_ready, b + 1)
                    dve.scalar_tensor_tensor(xt[s], xn[s], sm[:, s, 6:7], xt[s], ALU.mult, ALU.add)\
                       .then_inc(x3_ready, 1)
                for b in batches:
                    s = b % GB
                    dve.wait_ge(x3_ready, b + 1)
                    for half in range(2):
                        n = TAIL_AT[("mix", b, half)]
                        part = xt[s][:, half * 512:(half + 1) * 512]
                        dve.wait_ge(tail_full, n + 1)
                        dve.tensor_tensor(part, part, TB[n % 6][0:L, :], ALU.add).then_inc(mixed, 1)


def kernel(**inputs):
    import numpy as np
    import concourse.bacc as bacc
    from concourse.bass_utils import run_bass_kernel_spmd

    a = {k: np.asarray(v) for k, v in inputs.items()}

    def tiles(w, rows):
        o, i = w.shape
        return w.reshape(o // rows, rows, i // 1024, 8, P).transpose(0, 2, 4, 3, 1).reshape(-1, P, 8 * rows)

    def channels(v):
        return v.reshape(NI, P, -1).transpose(1, 0, 2)

    arrays = {
        "x": a["x"],
        "ctx": a["ctx_4096"],
        "ctx_t": a["ctx_4096"].reshape(B, SK, NK, P).transpose(0, 3, 2, 1),
        "w_in": tiles(a["L0_attn_W_in"], P),
        "w_out": tiles(a["L0_attn_W_out"], P),
        "w_x": tiles(a["L0_attn_W_x"], SSM),
        "w_dt": a["L0_attn_W_dt"].T,
        "conv_w": channels(a["L0_attn_conv_w"]),
        "conv_b": channels(a["L0_attn_conv_b"])[:, :, 0],
        "b_dt": channels(a["L0_attn_b_dt"])[:, :, 0],
        "a_log": channels(a["L0_attn_A_log"]),
        "d_skip": channels(a["L0_attn_D"])[:, :, 0],
        "w_router": a["L0_ffn_router_weight"].reshape(E, NK, P).transpose(2, 1, 0),
        "b_router": a["L0_ffn_router_bias"].reshape(1, E),
        "e_bias": a["L0_ffn_expert_bias"],
    }
    arrays = {k: np.ascontiguousarray(v) for k, v in arrays.items()}
    nc = bacc.Bacc("TRN2", target_bir_lowering=False, num_devices=1)
    args = [nc.dram_tensor(k, v.shape, F32, kind="ExternalInput").ap() for k, v in arrays.items()]
    args.append(nc.dram_tensor("out", (B, L, H), F32, kind="ExternalOutput").ap())
    decoder_layer(nc, *args)
    r = run_bass_kernel_spmd(nc, [arrays], core_ids=[0])
    return r.results[0]["out"]
```
